# Optimizing a Trainium2 kernel written in Bass

```python
import numpy as np
import jax
import jax.numpy as jnp

def _softmax(x, axis=-1):
    return jax.nn.softmax(x, axis=axis)

def _gelu(x):
    return jax.nn.gelu(x, approximate=True)

def _silu(x):
    return jax.nn.silu(x)

def _sigmoid(x):
    return jax.nn.sigmoid(x)

def _layernorm(x, axis=-1, eps=1e-05):
    m = jnp.mean(x, axis=axis, keepdims=True)
    v = jnp.var(x, axis=axis, keepdims=True)
    return (x - m) / jnp.sqrt(v + eps)

def _scatter_add(tgt, idx, src, axis=0):
    return tgt.at[idx].add(src)

def _segment_sum(src, seg, n):
    return jax.ops.segment_sum(src, seg, n)
kernel_name = 'mk_flamingo_gated_d2_seqx_r8_c8e363'

def setup_inputs(seed: int=0):
    np.random.seed(seed)
    _w = jnp.asarray

    def _rec_inputs():
        import jax
        import jax.numpy as jnp
        _rk = jax.random.key(seed)
        x = 7.22e-05 + 1 * jax.random.normal(jax.random.fold_in(_rk, 1), (4, 256, 256), jnp.float32)
        _lenS = 256 - jax.random.randint(jax.random.fold_in(_rk, 7), (4,), 0, max(1, 256 // 4) + 1, jnp.int32)
        _lenS2 = 256 - jax.random.randint(jax.random.fold_in(_rk, 8), (4,), 0, max(1, 256 // 4) + 1, jnp.int32)
        _ctx_1024P = jax.random.normal(jax.random.fold_in(_rk, 11), (4, 16, 128), jnp.float32)
        _ctx_1024c = jax.random.dirichlet(jax.random.fold_in(_rk, 511), 0.3 * jnp.ones((16,), jnp.float32), (4, 256))
        _ctx_1024t = jnp.einsum('bsk,bkd->bsd', _ctx_1024c, _ctx_1024P)
        _ctx_1024t = _ctx_1024t * jax.lax.rsqrt(jnp.mean(jnp.square(_ctx_1024t)) + 1e-12) * 0.953939
        ctx_1024 = 2.81802e-05 + 1.00001 * (_ctx_1024t + 0.3 * jax.random.normal(jax.random.fold_in(_rk, 611), (4, 256, 128), jnp.float32))
        _g = jax.random.normal(jax.random.fold_in(_rk, 9001), (2, 2), jnp.float32)
        _g = jnp.sign(_g) * jnp.maximum(jnp.abs(_g), 1.0) + (_g == 0) * 1.0
        g_xattn = _g[0]
        g_ffn = _g[1]
        return (x, ctx_1024, g_xattn, g_ffn)
    x, ctx_1024, g_xattn, g_ffn = _rec_inputs()

    def _L0_xattn_setup():
        import jax, jax.numpy as jnp
        import numpy as np
        key = jax.random.key(seed)
        ks = jax.random.split(key, 6)
        B, L, N, C, D = (8, 64, 256, 128, 128)
        return {'teacher_logits': jax.random.normal(ks[0], (B, L, N), dtype=jnp.float32), 'teacher_features': jax.random.normal(ks[1], (B, N, C), dtype=jnp.float32), 'Wq': jax.random.normal(ks[2], (D, C), dtype=jnp.float32) * (1.0 / np.sqrt(C)), 'bq': jnp.zeros((D,), dtype=jnp.float32), 'Wk': jax.random.normal(ks[3], (D, C), dtype=jnp.float32) * (1.0 / np.sqrt(C)), 'bk': jnp.zeros((D,), dtype=jnp.float32)}
    _L0_xattn_all = _L0_xattn_setup()
    _L0_xattn_in = {k: v for k, v in _L0_xattn_all.items() if k in ('Wq', 'bq', 'Wk', 'bk')}
    del _L0_xattn_all

    def _L0_ffn_setup():
        import jax, jax.numpy as jnp
        import numpy as np
        HIDDEN = 256
        INTER = 704
        B, S = (2, 256)

        def _ternary(key, shape):
            return jax.random.randint(key, shape, -1, 2).astype(jnp.float32)
        key = jax.random.key(seed)
        ks = jax.random.split(key, 7)
        x = jax.random.normal(ks[0], (B, S, HIDDEN), dtype=jnp.float32)
        gate_w = _ternary(ks[1], (INTER, HIDDEN))
        up_w = _ternary(ks[2], (INTER, HIDDEN))
        down_w = _ternary(ks[3], (HIDDEN, INTER))
        gate_s = jax.random.uniform(ks[4], (INTER,), minval=0.01, maxval=0.1, dtype=jnp.float32)
        up_s = jax.random.uniform(ks[5], (INTER,), minval=0.01, maxval=0.1, dtype=jnp.float32)
        down_s = jax.random.uniform(ks[6], (HIDDEN,), minval=0.01, maxval=0.1, dtype=jnp.float32)
        return {'x': x, 'gate_w': gate_w, 'up_w': up_w, 'down_w': down_w, 'gate_s': gate_s, 'up_s': up_s, 'down_s': down_s}
    _L0_ffn_all = _L0_ffn_setup()
    _L0_ffn_in = {k: v for k, v in _L0_ffn_all.items() if k in ('gate_w', 'up_w', 'down_w', 'gate_s', 'up_s', 'down_s')}
    del _L0_ffn_all

    def _L1_xattn_setup():
        import jax, jax.numpy as jnp
        import numpy as np
        import math
        B, L, DM = (2, 256, 128)
        DS, DC, EXP = (16, 4, 2)
        DI = EXP * DM
        DR = math.ceil(DM / 16)
        DT_MIN, DT_MAX, DT_FLOOR = (0.001, 0.1, 0.0001)

        def _ssm_forward(hidden_states, z, in_proj_w, conv_w, conv_b, x_proj_w, dt_proj_w, dt_proj_b, A_log, D):
            b = hidden_states.shape[0]
            x = jnp.einsum('ed,bld->bel', in_proj_w, hidden_states)
            xp = jnp.pad(x, ((0, 0), (0, 0), (DC - 1, 0)))
            xc = jax.lax.conv_general_dilated(xp, conv_w[:, None, :], window_strides=(1,), padding='VALID', dimension_numbers=('NCH', 'OIH', 'NCH'), feature_group_count=DI)
            u = jax.nn.silu(xc + conv_b[None, :, None])
            x_dbl = jnp.einsum('ke,bel->bkl', x_proj_w, u)
            dt_lo = x_dbl[:, :DR]
            Bm = x_dbl[:, DR:DR + DS]
            Cm = x_dbl[:, DR + DS:]
            delta = jax.nn.softplus(jnp.einsum('er,brl->bel', dt_proj_w, dt_lo) + dt_proj_b[None, :, None])
            A = -jnp.exp(A_log)

            def step(state, xs):
                d_t, B_t, C_t, u_t = xs
                dA = jnp.exp(d_t[..., None] * A)
                state = state * dA + (d_t * u_t)[..., None] * B_t[:, None, :]
                y_t = jnp.einsum('ben,bn->be', state, C_t)
                return (state, y_t)
            xs = (jnp.moveaxis(delta, -1, 0), jnp.moveaxis(Bm, -1, 0), jnp.moveaxis(Cm, -1, 0), jnp.moveaxis(u, -1, 0))
            state0 = jnp.zeros((b, DI, DS), delta.dtype)
            _, ys = jax.lax.scan(step, state0, xs)
            y = jnp.moveaxis(ys, 0, -1)
            y = y + D[None, :, None] * u
            y = y * jax.nn.silu(z)
            return jnp.swapaxes(y, 1, 2)
        key = jax.random.key(seed)
        ks = jax.random.split(key, 8)
        hidden_states = jax.random.normal(ks[0], (B, L, DM), jnp.float32)
        z = jax.random.normal(ks[1], (B, DI, L), jnp.float32)
        in_proj_w = jax.random.normal(ks[2], (DI, DM), jnp.float32) * DM ** (-0.5)
        conv_w = jax.random.normal(ks[3], (DI, DC), jnp.float32) * DC ** (-0.5)
        conv_b = jnp.zeros((DI,), jnp.float32)
        x_proj_w = jax.random.normal(ks[4], (DR + 2 * DS, DI), jnp.float32) * DI ** (-0.5)
        dt_std = DR ** (-0.5)
        dt_proj_w = jax.random.uniform(ks[5], (DI, DR), jnp.float32, -dt_std, dt_std)
        dt = jnp.exp(jax.random.uniform(ks[6], (DI,), jnp.float32) * (math.log(DT_MAX) - math.log(DT_MIN)) + math.log(DT_MIN))
        dt = jnp.clip(dt, DT_FLOOR)
        dt_proj_b = dt + jnp.log(-jnp.expm1(-dt))
        A_log = jnp.log(jnp.broadcast_to(jnp.arange(1, DS + 1, dtype=jnp.float32), (DI, DS)))
        D = jnp.ones((DI,), jnp.float32)
        return dict(hidden_states=hidden_states, z=z, in_proj_w=in_proj_w, conv_w=conv_w, conv_b=conv_b, x_proj_w=x_proj_w, dt_proj_w=dt_proj_w, dt_proj_b=dt_proj_b, A_log=A_log, D=D)
    _L1_xattn_all = _L1_xattn_setup()
    _L1_xattn_in = {k: v for k, v in _L1_xattn_all.items() if k in ('in_proj_w', 'conv_w', 'conv_b', 'x_proj_w', 'dt_proj_w', 'dt_proj_b', 'A_log', 'D')}
    del _L1_xattn_all

    def _L1_ffn_setup():
        import jax, jax.numpy as jnp
        import numpy as np
        B, T, D = (2, 128, 256)
        H, K, DK = (4, 8, 64)
        E = 2048
        NK = 128
        key = jax.random.key(seed)
        k1, k2, k3, k4, k5 = jax.random.split(key, 5)
        x = jax.random.normal(k1, (B, T, D), dtype=jnp.float32)
        Wq = jax.random.normal(k2, (D, 2 * H * DK), dtype=jnp.float32) * 0.02
        keys = jax.random.normal(k3, (H, NK, 2, DK), dtype=jnp.float32) * 0.02
        e_down = jax.random.normal(k4, (E, D), dtype=jnp.float32) * 0.01
        e_up = jax.random.normal(k5, (E, D), dtype=jnp.float32) * 0.01
        return {'x': x, 'Wq': Wq, 'keys': keys, 'e_down': e_down, 'e_up': e_up}
    _L1_ffn_all = _L1_ffn_setup()
    _L1_ffn_in = {k: v for k, v in _L1_ffn_all.items() if k in ('Wq', 'keys', 'e_down', 'e_up')}
    del _L1_ffn_all
    return {'x': x, 'ctx_1024': ctx_1024, 'g_xattn': g_xattn, 'g_ffn': g_ffn, 'L0_xattn_Wq': _L0_xattn_in['Wq'], 'L0_xattn_bq': _L0_xattn_in['bq'], 'L0_xattn_Wk': _L0_xattn_in['Wk'], 'L0_xattn_bk': _L0_xattn_in['bk'], 'L0_ffn_gate_w': _L0_ffn_in['gate_w'], 'L0_ffn_up_w': _L0_ffn_in['up_w'], 'L0_ffn_down_w': _L0_ffn_in['down_w'], 'L0_ffn_gate_s': _L0_ffn_in['gate_s'], 'L0_ffn_up_s': _L0_ffn_in['up_s'], 'L0_ffn_down_s': _L0_ffn_in['down_s'], 'L1_xattn_in_proj_w': _L1_xattn_in['in_proj_w'], 'L1_xattn_conv_w': _L1_xattn_in['conv_w'], 'L1_xattn_conv_b': _L1_xattn_in['conv_b'], 'L1_xattn_x_proj_w': _L1_xattn_in['x_proj_w'], 'L1_xattn_dt_proj_w': _L1_xattn_in['dt_proj_w'], 'L1_xattn_dt_proj_b': _L1_xattn_in['dt_proj_b'], 'L1_xattn_A_log': _L1_xattn_in['A_log'], 'L1_xattn_D': _L1_xattn_in['D'], 'L1_ffn_Wq': _L1_ffn_in['Wq'], 'L1_ffn_keys': _L1_ffn_in['keys'], 'L1_ffn_e_down': _L1_ffn_in['e_down'], 'L1_ffn_e_up': _L1_ffn_in['e_up']}

def reference(x, ctx_1024, g_xattn, g_ffn, L0_xattn_Wq, L0_xattn_bq, L0_xattn_Wk, L0_xattn_bk, L0_ffn_gate_w, L0_ffn_up_w, L0_ffn_down_w, L0_ffn_gate_s, L0_ffn_up_s, L0_ffn_down_s, L1_xattn_in_proj_w, L1_xattn_conv_w, L1_xattn_conv_b, L1_xattn_x_proj_w, L1_xattn_dt_proj_w, L1_xattn_dt_proj_b, L1_xattn_A_log, L1_xattn_D, L1_ffn_Wq, L1_ffn_keys, L1_ffn_e_down, L1_ffn_e_up):
    import jax
    import jax.numpy as jnp

    def _L0_xattn_ref(teacher_logits, teacher_features, Wq, bq, Wk, bk):
        import jax, jax.numpy as jnp
        import numpy as np
        query = jnp.einsum('bnc,dc->bnd', teacher_features, Wq) + bq
        key = jnp.einsum('bnc,dc->bnd', teacher_features, Wk) + bk
        energy = jnp.einsum('bnd,bmd->bnm', query, key)
        attention = jax.nn.softmax(energy, axis=-1)
        x_m = jnp.einsum('bln,bmn->blm', teacher_logits, attention)
        return x_m

    def _L0_ffn_ref(x, gate_w, up_w, down_w, gate_s, up_s, down_s):
        import jax, jax.numpy as jnp
        import numpy as np
        HIDDEN = 256
        INTER = 704
        B, S = (2, 256)

        def _ternary(key, shape):
            return jax.random.randint(key, shape, -1, 2).astype(jnp.float32)
        b, s, h = x.shape
        xf = x.reshape(b * s, h)
        g = jnp.einsum('th,ih->ti', xf, gate_w) * gate_s
        u = jnp.einsum('th,ih->ti', xf, up_w) * up_s
        hdn = jax.nn.silu(g) * u
        out = jnp.einsum('ti,hi->th', hdn, down_w) * down_s
        return out.reshape(b, s, -1)

    def _L1_xattn_ref(hidden_states, z, in_proj_w, conv_w, conv_b, x_proj_w, dt_proj_w, dt_proj_b, A_log, D):
        import jax, jax.numpy as jnp
        import numpy as np
        import math
        B, L, DM = (2, 256, 128)
        DS, DC, EXP = (16, 4, 2)
        DI = EXP * DM
        DR = math.ceil(DM / 16)
        DT_MIN, DT_MAX, DT_FLOOR = (0.001, 0.1, 0.0001)

        def _ssm_forward(hidden_states, z, in_proj_w, conv_w, conv_b, x_proj_w, dt_proj_w, dt_proj_b, A_log, D):
            b = hidden_states.shape[0]
            x = jnp.einsum('ed,bld->bel', in_proj_w, hidden_states)
            xp = jnp.pad(x, ((0, 0), (0, 0), (DC - 1, 0)))
            xc = jax.lax.conv_general_dilated(xp, conv_w[:, None, :], window_strides=(1,), padding='VALID', dimension_numbers=('NCH', 'OIH', 'NCH'), feature_group_count=DI)
            u = jax.nn.silu(xc + conv_b[None, :, None])
            x_dbl = jnp.einsum('ke,bel->bkl', x_proj_w, u)
            dt_lo = x_dbl[:, :DR]
            Bm = x_dbl[:, DR:DR + DS]
            Cm = x_dbl[:, DR + DS:]
            delta = jax.nn.softplus(jnp.einsum('er,brl->bel', dt_proj_w, dt_lo) + dt_proj_b[None, :, None])
            A = -jnp.exp(A_log)

            def step(state, xs):
                d_t, B_t, C_t, u_t = xs
                dA = jnp.exp(d_t[..., None] * A)
                state = state * dA + (d_t * u_t)[..., None] * B_t[:, None, :]
                y_t = jnp.einsum('ben,bn->be', state, C_t)
                return (state, y_t)
            xs = (jnp.moveaxis(delta, -1, 0), jnp.moveaxis(Bm, -1, 0), jnp.moveaxis(Cm, -1, 0), jnp.moveaxis(u, -1, 0))
            state0 = jnp.zeros((b, DI, DS), delta.dtype)
            _, ys = jax.lax.scan(step, state0, xs)
            y = jnp.moveaxis(ys, 0, -1)
            y = y + D[None, :, None] * u
            y = y * jax.nn.silu(z)
            return jnp.swapaxes(y, 1, 2)
        return _ssm_forward(hidden_states, z, in_proj_w, conv_w, conv_b, x_proj_w, dt_proj_w, dt_proj_b, A_log, D)

    def _L1_ffn_ref(x, Wq, keys, e_down, e_up):
        import jax, jax.numpy as jnp
        import numpy as np
        B, T, D = (2, 128, 256)
        H, K, DK = (4, 8, 64)
        E = 2048
        NK = 128
        b, t, d = x.shape
        q = (x @ Wq).reshape(b, t, H, 2, DK)
        q1, q2 = (q[..., 0, :], q[..., 1, :])
        sim1 = jnp.einsum('bthd,hkd->bthk', q1, keys[:, :, 0, :])
        sim2 = jnp.einsum('bthd,hkd->bthk', q2, keys[:, :, 1, :])
        s1, i1 = jax.lax.top_k(sim1, K)
        s2, i2 = jax.lax.top_k(sim2, K)
        all_scores = (s1[..., :, None] + s2[..., None, :]).reshape(b, t, H, K * K)
        all_indices = (i1[..., :, None] * NK + i2[..., None, :]).reshape(b, t, H, K * K)
        final_scores, pk_idx = jax.lax.top_k(all_scores, K)
        final_indices = jnp.take_along_axis(all_indices, pk_idx, axis=-1)
        w_down = e_down[final_indices]
        w_up = e_up[final_indices]
        hidden = jnp.einsum('btd,bthkd->bthk', x, w_down)
        hidden = jax.nn.silu(hidden)
        hidden = hidden * jax.nn.relu(final_scores)
        out = jnp.einsum('bthk,bthkd->btd', hidden, w_up)
        return out
    x = x + jnp.tanh(g_xattn[0]) * _L0_xattn_ref(_layernorm(x, axis=-1), ctx_1024, L0_xattn_Wq, L0_xattn_bq, L0_xattn_Wk, L0_xattn_bk)
    x = x + jnp.tanh(g_ffn[0]) * _L0_ffn_ref(_layernorm(x, axis=-1), L0_ffn_gate_w, L0_ffn_up_w, L0_ffn_down_w, L0_ffn_gate_s, L0_ffn_up_s, L0_ffn_down_s)
    x = x + jnp.tanh(g_xattn[1]) * _L1_xattn_ref(ctx_1024, _layernorm(x, axis=-1), L1_xattn_in_proj_w, L1_xattn_conv_w, L1_xattn_conv_b, L1_xattn_x_proj_w, L1_xattn_dt_proj_w, L1_xattn_dt_proj_b, L1_xattn_A_log, L1_xattn_D)
    x = x + jnp.tanh(g_ffn[1]) * _L1_ffn_ref(_layernorm(x, axis=-1), L1_ffn_Wq, L1_ffn_keys, L1_ffn_e_down, L1_ffn_e_up)
    return x

_drawn_inputs = setup_inputs


def setup_inputs(seed=0):
    import zlib

    import numpy as np

    out = dict(_drawn_inputs(seed))
    spreads = {'g_ffn': (-1.0, 0.6),
     'L0_xattn_bq': (0.0, 0.1),
     'L0_xattn_bk': (0.0, 0.8),
     'L1_xattn_conv_b': (0.0, 0.306),
     'L1_xattn_D': (1.0, 0.2)}
    factors = {'L1_xattn_dt_proj_w': 7.363,
     'L1_xattn_dt_proj_b': 3.027,
     'L1_xattn_A_log': 2.979,
     'L1_ffn_Wq': 8.0,
     'L1_ffn_keys': 8.0,
     'L1_ffn_e_down': 8.0,
     'L1_ffn_e_up': 8.0}
    for name, (base, spread) in spreads.items():
        noise = np.random.default_rng([zlib.crc32(name.encode()), seed]).standard_normal(out[name].shape)
        drawn = base * np.exp(spread * noise) if base else spread * noise
        out[name] = jnp.asarray(drawn.astype(out[name].dtype))
    for name, factor in factors.items():
        out[name] = (out[name] * factor).astype(out[name].dtype)
    return out
```

```python
import numpy as np
import concourse.bass as bass
from concourse import mybir
from contextlib import ExitStack

P = 128
B, S, D = 4, 256, 256
CTX = 128
T = B * S
NT = T // P
TB = S // P
DK_F = D // P
INTER = 704
NI = (INTER + P - 1) // P
LAST = INTER - (NI - 1) * P
DI, DS, DC, DR = 256, 16, 4, 8
NC = DI // P
XD = DR + 2 * DS
H, K, DK, NK, E = 4, 8, 64, 128, 2048
ROWS = E // NK
HK = H * K
EPS = 1e-5
NPB = DS // B
UNITS = NPB * NC
SLOTS = 4
PAD = S + DC - 1
PARTS = 3


def build(nc, io, out):
    f32, b16, u32, i32 = mybir.dt.float32, mybir.dt.bfloat16, mybir.dt.uint32, mybir.dt.int32
    ALU, ACT, AX = mybir.AluOpType, mybir.ActivationFunctionType, mybir.AxisListType
    ds = bass.ds
    ctx = ExitStack()
    with ctx:
        def sb(name, shape, dt=f32):
            return ctx.enter_context(nc.sbuf_tensor("sb_" + name, shape, dt))

        def sem(name):
            return ctx.enter_context(nc.semaphore(name))

        x = sb("x", [P, NT * D])
        ctxT = sb("ctxT", [P, T])
        wqT, wkT = sb("wqT", [P, P]), sb("wkT", [P, P])
        bq, bk = sb("bq", [P, 1]), sb("bk", [P, 1])
        gate_w, up_w = sb("gate_w", [P, DK_F, INTER]), sb("up_w", [P, DK_F, INTER])
        down_w = sb("down_w", [P, NI, D])
        gate_s, up_s, half_gs = sb("gate_s", [P, NI]), sb("up_s", [P, NI]), sb("half_gs", [P, NI])
        down_s, dsg = sb("down_s", [P, D]), sb("dsg", [P, D])
        in_w = sb("in_w", [P, DI])
        conv_w, conv_b = sb("conv_w", [P, NC, DC]), sb("conv_b", [P, NC])
        xp_w = sb("xp_w", [P, NC, XD])
        dt_w, dt_b = sb("dt_w", [DR, DI]), sb("dt_b", [P, NC])
        A = sb("A", [P, NC * DS])
        Dp = sb("Dp", [P, NC])
        wqp = sb("wqp", [P, DK_F, H * P])
        keysT = sb("keysT", [P, H, NK])
        e_down = sb("e_down", [P, DK_F, E])
        e_up = sb("e_up", [P, ROWS, D])
        gains = sb("gains", [P, 4])
        ident = sb("ident", [P, P])
        ident_d = sb("ident_d", [P, NC, P])
        iota_i = sb("iota_i", [P, P], i32)
        iota_b = sb("iota_b", [P, P], b16)
        iota_f = sb("iota_f", [P, K])
        minus_half = sb("minus_half", [P, NT])
        stats = sb("stats", [P, NT, 6])
        mv = sb("mv", [P, NT, 2])
        mean = sb("mean", [P, NT])
        veps, rstd = sb("veps", [P, NT]), sb("rstd", [P, NT])
        xl = sb("xl", [P, TB, D])
        xlT = sb("xlT", [P, DK_F, S])
        qT, kT = sb("qT", [P, S]), sb("kT", [P, S])
        neg_max, row_sum, row_inv = sb("neg_max", [P, TB]), sb("row_sum", [P, TB]), sb("row_inv", [P, TB])
        att = sb("att", [P, TB, S])
        attT = sb("attT", [P, TB, S])
        th = sb("th", [P, 2, S])
        ga = sb("ga", [P, 2, S])
        hdn = sb("hdn", [P, NI, S])
        ffn = sb("ffn", [P, TB * D])
        u = sb("u", [P, NC, T])
        delta = sb("delta", [P, NC, T])
        du = sb("du", [P, NC, T])
        xdbl = sb("xdbl", [XD, T])
        y = delta
        arena = sb("arena", [P, 18 * T])
        xpad = arena[:, 0:NC * B * PAD].rearrange("p (c b s) -> p c b s", c=NC, b=B)
        conv = arena[:, 3 * T:5 * T].rearrange("p (c b s) -> p c b s", c=NC, b=B)
        sp_v = arena[:, 5 * T:7 * T].rearrange("p (c t) -> p c t", c=NC)
        sp_e = arena[:, 7 * T:9 * T].rearrange("p (c t) -> p c t", c=NC)
        sp_w = arena[:, 9 * T:11 * T].rearrange("p (c t) -> p c t", c=NC)
        sp_l = arena[:, 11 * T:13 * T].rearrange("p (c t) -> p c t", c=NC)
        sp_i = arena[:, 13 * T:15 * T].rearrange("p (c t) -> p c t", c=NC)
        dA = arena[:, 0:4 * T].rearrange("p (s t) -> p s t", s=SLOTS)
        dBu = arena[:, 4 * T:8 * T].rearrange("p (s t) -> p s t", s=SLOTS)
        hs = arena[:, 8 * T:10 * T].rearrange("p (s t) -> p s t", s=2)
        hc = arena[:, 10 * T:14 * T].rearrange("p (s t) -> p s t", s=SLOTS)
        bbc = arena[:, 14 * T:16 * T].rearrange("p (s t) -> p s t", s=2)
        cbc = arena[:, 16 * T:18 * T].rearrange("p (s t) -> p s t", s=2)
        GT = arena[:, 0:4 * T].rearrange("p (r t) -> p r t", r=ROWS)
        Y = arena[:, 4 * T:8 * T].bitcast(b16).rearrange("p (s j k) -> p s j k", s=TB, k=NK)
        GW = arena[:, 8 * T:10 * T].rearrange("p (r t) -> p r t", r=ROWS)
        sims = arena[:, 10 * T:12 * T].rearrange("p (s n k) -> p s n k", s=TB, k=NK)
        XW = arena[:, 12 * T:12 * T + TB * PARTS * 256].bitcast(b16).rearrange(
            "p (s q j r) -> p s q j r", s=TB, q=PARTS, r=ROWS)
        xnT = arena[:, 14 * T:14 * T + DK_F * S].rearrange("p (k t) -> p k t", k=DK_F)
        qTp = arena[:, 15 * T:16 * T].rearrange("p (h t) -> p h t", h=H)
        sz = arena[:, 16 * T:16 * T + 512].rearrange("p (c s) -> p c s", c=NC)
        yz = arena[:, 16 * T + 512:17 * T].rearrange("p (c s) -> p c s", c=NC)
        fin = arena[:, 17 * T:17 * T + TB * D].rearrange("p (s d) -> p s d", s=TB)
        NS = 2 * H
        top = sb("top", [P, NS, K])
        topi = sb("topi", [P, NS, K], u32)
        topf = sb("topf", [P, NS, K])
        cand = sb("cand", [P, H, K, K])
        best = sb("best", [P, H, K])
        pk = sb("pk", [P, H, K], u32)
        pab = sb("pab", [P, 2, HK], u32)
        pabf = sb("pabf", [P, 2 * HK])
        eq = sb("eq", [P, NS, K, K])
        picked = sb("picked", [P, 2 * HK])
        over = sb("over", [P, HK])
        V = sb("V", [P, 2 + PARTS, HK])
        part = sb("part", [P, HK], b16)
        rest = sb("rest", [P, HK])
        VT = sb("VT", [P, 2 + PARTS, HK])
        VTb = sb("VTb", [P, 2 + PARTS, HK], b16)
        onehot1 = sb("onehot1", [P, HK, ROWS], b16)

        ps = ctx.enter_context(nc.psum_tensor("ps", [P, 8, 512], f32))
        y_ps = ps[:, 0:4, :].rearrange("p (c h) s -> p c (h s)", c=NC)
        front_ps = y_ps
        T_ps = ps[:, 4, :].rearrange("p (k s) -> p k s", k=2)
        mm_ps = ps[:, 5, :].rearrange("p (k s) -> p k s", k=2)
        out_ps = (ps[:, 7, 0:D], ps[:, 4, 0:D])
        W_ps = ps[:, 0:4, :].rearrange("p g (j r) -> p (g j) r", r=ROWS)

        scratch = nc.dram_tensor("bc_scratch", [2 * DS, T], f32, kind="Internal").ap()

        ld_x, ld_front, ld_small, ld_attn, ld_ffn = (sem("ld_" + n) for n in ("x", "front", "small", "attn", "ffn"))
        ld_keys, ld_exp = sem("ld_keys"), sem("ld_exp")
        consts_ready, iota_ready, pads_ready = sem("consts_ready"), sem("iota_ready"), sem("pads_ready")
        dve_step, act_step, pool_step = sem("dve_step"), sem("act_step"), sem("pool_step")
        ga_scaled, w_part, d_ready = sem("ga_scaled"), sem("w_part"), sem("d_ready")
        dve_passed, pool_passed = sem("dve_passed"), sem("pool_passed")
        veps_ready, rstd_ready = sem("veps_ready"), sem("rstd_ready")
        gains_ready = sem("gains_ready")
        in_ps, xpad_ready, conv_ready, u_ready = sem("in_ps"), sem("xpad_ready"), sem("conv_ready"), sem("u_ready")
        xd_ps, xd_ready, xd_stored, dt_ps = sem("xd_ps"), sem("xd_ready"), sem("xd_stored"), sem("dt_ps")
        spv_ready, spe_ready, spw_ready = sem("spv_ready"), sem("spe_ready"), sem("spw_ready")
        spl_ready, spi_ready, a_ready = sem("spl_ready"), sem("spi_ready"), sem("a_ready")
        delta_ready, du_ready = sem("delta_ready"), sem("du_ready")
        b_loaded = [sem("b_loaded0"), sem("b_loaded1")]
        c_loaded = [sem("c_loaded0"), sem("c_loaded1")]
        da_ready, dbu_ready, scanned, hc_ready, y_added = (sem(n) for n in (
            "da_ready", "dbu_ready", "scanned", "hc_ready", "y_added"))
        xl_ready, xlT_ps, xlT_ready = sem("xl_ready"), sem("xlT_ps"), sem("xlT_ready")
        qk_ps, qk_ready, e_ps, max_ready, exp_ready = (sem(n) for n in (
            "qk_ps", "qk_ready", "e_ps", "max_ready", "exp_ready"))
        att_ready, attT_ps, attT_ready, xm_ps = (sem(n) for n in ("att_ready", "attT_ps", "attT_ready", "xm_ps"))
        xl2_ready, xl2T_ps, xl2T_ready = sem("xl2_ready"), sem("xl2T_ps"), sem("xl2T_ready")
        gu_ps, gate_act, hdn_ready, down_ps, x2_ready = (sem(n) for n in (
            "gu_ps", "gate_act", "hdn_ready", "down_ps", "x2_ready"))
        y_ready, zl_ready, sz_ready, yz_ready, yzT_ps = (sem(n) for n in (
            "y_ready", "zl_ready", "sz_ready", "yz_ready", "yzT_ps"))
        xn_ready, xnT_ps, xnT_ready = sem("xn_ready"), sem("xnT_ps"), sem("xnT_ready")
        q_ps, q_ready, sim_ps, sim_ready, g_ps, g_ready = (sem(n) for n in (
            "q_ps", "q_ready", "sim_ps", "sim_ready", "g_ps", "g_ready"))
        xy_ready, w_ps, gw_ready, up_ps, fin_ready, stored = (sem(n) for n in (
            "xy_ready", "w_ps", "gw_ready", "up_ps", "fin_ready", "stored"))

        block = ctx.enter_context(nc.Block())

        class Tally:

            def __init__(self):
                self.fixed, self.inner, self.base = 0, 0, 0

            def add(self):
                self.inner += 1

            def now(self):
                return self.base + self.fixed + self.inner

            def enter(self, i, per):
                self.fixed += self.inner
                self.inner, self.base, self.per = 0, i * per, per

            def leave(self, trips):
                assert self.inner == self.per, self.inner
                self.fixed += trips * self.per
                self.inner, self.base = 0, 0

        def chunk(i):
            return P if i < NI - 1 else LAST

        @block.sync
        def _(sp):
            sp.dma_start(ctxT[:, :], io["ctxT"]).then_inc(ld_front, 16)
            sp.dma_start(in_w[:, :], io["in_wT"]).then_inc(ld_front, 16)
            sp.dma_start(x[:, :].rearrange("p (t d) -> p t d", d=D),
                         io["x"].rearrange("(t p) d -> p t d", p=P)).then_inc(ld_x, 16)
            sp.dma_start(wqT[:, :], io["wqT"]).then_inc(ld_attn, 16)
            sp.dma_start(wkT[:, :], io["wkT"]).then_inc(ld_attn, 16)
            sp.dma_start(bq[:, :], io["bq"]).then_inc(ld_attn, 16)
            sp.dma_start(bk[:, :], io["bk"]).then_inc(ld_attn, 16)
            sp.dma_start(gate_w[:, :, :], io["gate_wT"].rearrange("(k p) n -> p k n", p=P)).then_inc(ld_ffn, 16)
            sp.dma_start(up_w[:, :, :], io["up_wT"].rearrange("(k p) n -> p k n", p=P)).then_inc(ld_ffn, 16)
            full = (NI - 1) * P
            sp.dma_start(down_w[:, 0:NI - 1, :], io["down_wT"][0:full, :].rearrange("(k p) n -> p k n", p=P)).then_inc(ld_ffn, 16)
            sp.dma_start(down_w[0:LAST, NI - 1, :], io["down_wT"][full:INTER, :]).then_inc(ld_ffn, 16)
            sp.wait_ge(xd_ready, T // 512)
            sp.dma_start(scratch, xdbl[DR:XD, :]).then_inc(xd_stored, 16)
            sp.wait_ge(xd_stored, 16)

            def spread(row_b, row_c, slot):
                sp.dma_start(bbc[:, slot, :], scratch[row_b, :].broadcast_to([P, T])).then_inc(b_loaded[slot], 16)
                sp.dma_start(cbc[:, slot, :], scratch[row_c, :].broadcast_to([P, T])).then_inc(c_loaded[slot], 16)

            sp.wait_ge(delta_ready, NC)
            spread(slice(0, 1), slice(DS, DS + 1), 0)
            spread(slice(1, 2), slice(DS + 1, DS + 2), 1)
            with sp.Fori(0, DS // 2 - 1) as m:
                for slot in range(2):
                    sp.wait_ge(dbu_ready, m * (2 * NC) + NC * (slot + 1))
                    sp.wait_ge(hc_ready, m * (2 * NC) + NC * (slot + 1))
                    spread(ds(m * 2 + 2 + slot, 1), ds(m * 2 + 2 + slot + DS, 1), slot)
            sp.sem_inc(stored, 1)
            with sp.Fori(0, B) as b:
                sp.wait_ge(fin_ready, b * TB + TB)
                sp.dma_start(out.rearrange("(t p) d -> p t d", p=P)[:, ds(b * TB, TB), :], fin).then_inc(stored, 16)
            sp.wait_ge(stored, 16 * B + 1)

        @block.gpsimd
        def _(pool):
            pool.memset(xpad[:, :, :, 0:DC - 1], 0.0).then_inc(pads_ready, 1)
            pool.memset(minus_half[:, :], -0.5).then_inc(pool_step, 1)
            pool.memset(ident[:, :], 0.0).then_inc(pool_step, 1)
            pool.wait_ge(pool_step, 2)
            pool.affine_select(out=ident[:, :], in_=ident[:, :], compare_op=ALU.not_equal, fill=1.0,
                               base=0, pattern=[[-1, P]], channel_multiplier=1).then_inc(consts_ready, 1)
            pool.iota(iota_i[:, :], pattern=[[1, P]], base=0, channel_multiplier=0).then_inc(pool_step, 1)
            pool.wait_ge(pool_step, 3)
            pool.tensor_copy(iota_b[:, :], iota_i[:, :]).then_inc(iota_ready, 1)
            pool.tensor_copy(iota_f[:, :], iota_i[:, 0:K]).then_inc(iota_ready, 1)
            pool.dma_start(wqp[:, :, :], io["wqp"].rearrange("(k p) n -> p k n", p=P)).then_inc(ld_keys, 16)
            pool.dma_start(keysT[:, :, :], io["keysT"].rearrange("p (h k) -> p h k", h=H)).then_inc(ld_keys, 16)
            pool.dma_start(e_down[:, :, :], io["e_downT"].rearrange("(k p) n -> p k n", p=P)).then_inc(ld_exp, 16)
            pool.dma_start(e_up[:, :, :], io["e_up"].rearrange("(r p) n -> p r n", p=P)).then_inc(ld_exp, 16)

            def power(first, tiles, n):
                pool.wait_ge(veps_ready, n)
                pool.sem_inc(pool_passed, 1)
                pool.tensor_tensor(rstd[:, ds(first, tiles)], veps[:, ds(first, tiles)], minus_half[:, 0:tiles], ALU.pow)\
                    .then_inc(rstd_ready, 1)

            power(0, NT, 1)
            pool.wait_ge(du_ready, NC)
            with pool.Fori(0, B) as b:
                for k in range(UNITS):
                    state, c = k // NC, k % NC
                    pool.wait_ge(b_loaded[state % 2], b * (NPB // 2 * 16) + 16 * (state // 2 + 1))
                    pool.wait_ge(scanned, b * UNITS + k + 1)
                    pool.tensor_tensor(dBu[:, k % SLOTS, :], du[:, c, :], bbc[:, state % 2, :], ALU.mult)\
                        .then_inc(dbu_ready, 1)
                    if k == 5:
                        power(b * TB, TB, b * 2 + 2)
                power(b * TB, TB, b * 2 + 3)
            with pool.Fori(0, B) as b:
                power(b * TB, TB, b + 2 * B + 2)

        @block.scalar
        def _(act):
            act.dma_start(xp_w[:, :, :], io["xp_wT"].rearrange("(c p) n -> p c n", p=P)).then_inc(ld_small, 16)
            act.dma_start(dt_w[:, :], io["dt_wT"]).then_inc(ld_small, 16)
            act.dma_start(conv_w[:, :, :], io["conv_w"].rearrange("(c p) n -> p c n", p=P)).then_inc(ld_small, 16)
            for dst, name in ((conv_b, "conv_b"), (dt_b, "dt_b"), (Dp, "D")):
                act.dma_start(dst[:, :], io[name]).then_inc(ld_small, 16)
            act.dma_start(A[:, :].rearrange("p (c n) -> p c n", c=NC),
                          io["A_log"].rearrange("(c p) n -> p c n", p=P)).then_inc(ld_small, 16)
            act.dma_start(gains[:, :], io["gates"].broadcast_to([P, 4])).then_inc(ld_small, 16)
            act.dma_start(gate_s[:, :], io["gate_s"]).then_inc(ld_small, 16)
            act.dma_start(up_s[:, :], io["up_s"]).then_inc(ld_small, 16)
            act.dma_start(down_s[:, :], io["down_s"].broadcast_to([P, D])).then_inc(ld_small, 16)

            act.wait_ge(pads_ready, 1)
            for n in range(2 * NC):
                c, h = n // 2, n % 2
                act.wait_ge(in_ps, n + 1)
                act.copy(xpad[:, c, 2 * h:2 * h + 2, DC - 1:PAD],
                         front_ps[:, c, h * 512:h * 512 + 512].rearrange("p (b s) -> p b s", b=2)).then_inc(xpad_ready, 1)
            act.wait_ge(ld_small, 16 * 11)
            for c in range(NC):
                act.wait_ge(conv_ready, c + 1)
                act.activation(u[:, c, :].rearrange("p (b s) -> p b s", b=B), conv[:, c], ACT.Silu,
                               bias=conv_b[:, c:c + 1]).then_inc(u_ready, 1)
            act.activation(gains[:, :], gains[:, :], ACT.Tanh).then_inc(gains_ready, 1)
            act.activation(A[:, :], A[:, :], ACT.Exp).then_inc(act_step, 1)
            for h in range(T // 512):
                act.wait_ge(xd_ps, h + 1)
                act.copy(xdbl[:, h * 512:h * 512 + 512], ps[0:XD, 4 + h, :]).then_inc(xd_ready, 1)
            act.wait_ge(act_step, 1)
            act.mul(A[:, :], A[:, :], -1.0).then_inc(a_ready, 1)
            for c in range(NC):
                act.wait_ge(dt_ps, 2 * (c + 1))
                act.activation(sp_v[:, c, :], front_ps[:, c, :], ACT.Identity, bias=dt_b[:, c:c + 1]).then_inc(spv_ready, 1)
                act.wait_ge(spv_ready, c + 1)
                act.activation(sp_e[:, c, :], sp_v[:, c, :], ACT.Abs).then_inc(act_step, 1)
                act.wait_ge(act_step, c + 2)
                act.activation(sp_e[:, c, :], sp_e[:, c, :], ACT.Exp, scale=-1.0).then_inc(spe_ready, 1)
            for c in range(NC):
                act.wait_ge(spw_ready, c + 1)
                act.activation(sp_l[:, c, :], sp_w[:, c, :], ACT.Ln).then_inc(spl_ready, 1)
            for c in range(NC):
                act.wait_ge(spl_ready, c + 1)
                act.activation(sp_i[:, c, :], sp_l[:, c, :], ACT.Exp, scale=-1.0).then_inc(spi_ready, 1)

            act.wait_ge(a_ready, 1)
            act.wait_ge(delta_ready, NC)
            act.wait_ge(ld_attn, 64)
            with act.Fori(0, B) as b:
                def decay(k):
                    state, c = k // NC, k % NC
                    act.wait_ge(scanned, b * UNITS + k + 1)
                    act.activation(dA[:, k % SLOTS, :], delta[:, c, :], ACT.Exp,
                                   scale=A[:, ds(b * NPB + (c * DS + state), 1)]).then_inc(da_ready, 1)

                def gate(i):
                    m, s = chunk(i), i % 2
                    act.wait_ge(gu_ps, b * NI + i + 1)
                    if i >= 2:
                        act.wait_ge(hdn_ready, b * NI + i - 1)
                    act.activation(th[0:m, s, :], ps[0:m, 6 + s, 0:S], ACT.Tanh, scale=half_gs[0:m, i:i + 1])\
                        .then_inc(gate_act, 1)
                    act.activation(ga[0:m, s, :], ps[0:m, 6 + s, 0:S], ACT.Copy, scale=half_gs[0:m, i:i + 1])\
                        .then_inc(gate_act, 1)

                act.wait_ge(xlT_ps, b + 1)
                act.copy(xlT[:, :, :], T_ps).then_inc(xlT_ready, 1)
                act.wait_ge(qk_ps, b + 1)
                act.activation(qT[:, :], mm_ps[:, 0, :], ACT.Identity, bias=bq[:, :]).then_inc(qk_ready, 1)
                act.activation(kT[:, :], mm_ps[:, 1, :], ACT.Identity, bias=bk[:, :]).then_inc(qk_ready, 1)
                decay(0)
                decay(1)
                act.wait_ge(max_ready, b + 1)
                for m in range(TB):
                    act.activation(att[:, m, :], mm_ps[:, m, :], ACT.Exp, bias=neg_max[:, m:m + 1],
                                   accum_out=row_sum[:, m:m + 1]).then_inc(exp_ready, 1)
                decay(2)
                decay(3)
                act.wait_ge(attT_ps, b + 1)
                act.copy(attT[:, :, :], T_ps).then_inc(attT_ready, 1)
                decay(4)
                decay(5)
                act.wait_ge(xl2T_ps, b + 1)
                act.copy(xlT[:, :, :], T_ps).then_inc(xl2T_ready, 1)
                gate(0)
                gate(1)
                decay(6)
                gate(2)
                gate(3)
                decay(7)
                gate(4)
                gate(5)

            act.wait_ge(y_added, B * UNITS + SLOTS)
            for c in range(NC):
                act.copy(y[:, c, :], y_ps[:, c, :]).then_inc(y_ready, 1)
            with act.Fori(0, B) as b:
                act.wait_ge(zl_ready, b * TB + TB)
                act.activation(sz, xl[:, :, :], ACT.Silu).then_inc(sz_ready, 1)
                act.wait_ge(xnT_ps, b + 1)
                act.copy(xnT, T_ps).then_inc(xnT_ready, 1)
                for n in range(2):
                    act.wait_ge(q_ps, b * 2 + n + 1)
                    act.copy(qTp[:, 2 * n:2 * n + 2, :], ps[:, 5 + n, :].rearrange("p (h t) -> p h t", h=2)).then_inc(q_ready, 1)
                for s in range(TB):
                    for side in range(2):
                        act.wait_ge(sim_ps, b * 2 * TB + 2 * s + side + 1)
                        act.copy(sims[:, s, side * H:side * H + H, :],
                                 ps[:, 5 + side, :].rearrange("p (h k) -> p h k", h=H)).then_inc(sim_ready, 1)
                for n in range(ROWS // 2):
                    act.wait_ge(g_ps, b * (ROWS // 2) + n + 1)
                    act.activation(GT[:, 2 * n:2 * n + 2, :], ps[:, 5 + n % 2, :].rearrange("p (r t) -> p r t", r=2),
                                   ACT.Silu).then_inc(g_ready, 1)

        @block.vector
        def _(dve):
            steps = Tally()

            def step(instruction):
                instruction.then_inc(dve_step, 1)
                steps.add()

            def then():
                dve.wait_ge(dve_step, steps.now())

            def apart():
                dve.sem_inc(dve_passed, 1)

            def tile(i, n=1):
                return x[:, ds(i * D, n * D)] if not isinstance(i, int) else x[:, i * D:(i + n) * D]

            def sums(first, n):
                apart()
                for t in range(n):
                    step(dve.bn_stats(stats[:, t, :], tile(first + t)))
                then()
                apart()
                for t in range(n):
                    step(dve.bn_aggr(mv[:, t, :], stats[:, t, :]))
                then()
                apart()
                step(dve.tensor_copy(mean[:, ds(first, n)], mv[:, 0:n, 0]))
                dve.tensor_scalar(veps[:, ds(first, n)], mv[:, 0:n, 1], EPS, None, ALU.add).then_inc(veps_ready, 1)

            def normed(dst, i, n_rstd, signal):
                dve.wait_ge(rstd_ready, n_rstd)
                for t in range(TB):
                    dve.tensor_scalar(dst[:, t, :], tile(i + t), mean[:, ds(i + t, 1)], rstd[:, ds(i + t, 1)],
                                      ALU.subtract, ALU.mult).then_inc(signal, 1)

            dve.wait_ge(ld_small, 16 * 11)
            for c in range(NC):
                dve.wait_ge(xpad_ready, 2 * (c + 1))
                step(dve.tensor_scalar(conv[:, c], xpad[:, c, :, 0:S], conv_w[:, c, 0:1], None, ALU.mult))
                for k in range(1, DC):
                    then()
                    ins = dve.scalar_tensor_tensor(conv[:, c], xpad[:, c, :, k:k + S], conv_w[:, c, k:k + 1], conv[:, c],
                                                   ALU.mult, ALU.add)
                    if k < DC - 1:
                        step(ins)
                    else:
                        ins.then_inc(conv_ready, 1)
            dve.wait_ge(ld_x, 16)
            for t in range(NT):
                step(dve.bn_stats(stats[:, t, :], tile(t)))
            then()
            for t in range(NT):
                step(dve.bn_aggr(mv[:, t, :], stats[:, t, :]))
            then()
            step(dve.tensor_copy(mean[:, :], mv[:, :, 0]))
            dve.tensor_scalar(veps[:, :], mv[:, :, 1], EPS, None, ALU.add).then_inc(veps_ready, 1)
            dve.wait_ge(consts_ready, 1)
            for c in range(NC):
                dve.tensor_scalar(ident_d[:, c, :], ident[:, :], Dp[:, c:c + 1], None, ALU.mult).then_inc(d_ready, 1)
            step(dve.tensor_scalar(half_gs[:, :], gate_s[:, :], 0.5, None, ALU.mult))
            dve.wait_ge(gains_ready, 1)
            step(dve.tensor_scalar(dsg[:, :], down_s[:, :], gains[:, 2:3], None, ALU.mult))
            for c in range(NC):
                dve.wait_ge(spe_ready, c + 1)
                dve.tensor_scalar(sp_w[:, c, :], sp_e[:, c, :], 1.0, None, ALU.add).then_inc(spw_ready, 1)
            for c in range(NC):
                dve.wait_ge(spw_ready, c + 1)
                step(dve.scalar_tensor_tensor(sp_e[:, c, :], sp_w[:, c, :], 1.0, sp_e[:, c, :], ALU.subtract, ALU.subtract))
            for c in range(NC):
                dve.wait_ge(spi_ready, c + 1)
                then()
                step(dve.tensor_tensor(sp_i[:, c, :], sp_e[:, c, :], sp_i[:, c, :], ALU.mult))
                then()
                step(dve.tensor_tensor(sp_l[:, c, :], sp_l[:, c, :], sp_i[:, c, :], ALU.subtract))
                then()
                dve.scalar_tensor_tensor(delta[:, c, :], sp_v[:, c, :], 0.0, sp_l[:, c, :], ALU.max, ALU.add)\
                   .then_inc(delta_ready, 1)
            for c in range(NC):
                dve.wait_ge(delta_ready, c + 1)
                dve.tensor_tensor(du[:, c, :], delta[:, c, :], u[:, c, :], ALU.mult).then_inc(du_ready, 1)
            dve.wait_ge(du_ready, NC)
            dve.sem_inc(scanned, SLOTS)

            with dve.Fori(0, B) as b:
                steps.enter(b, 13)

                def scan(k):
                    dve.wait_ge(da_ready, b * UNITS + k + 1)
                    dve.wait_ge(dbu_ready, b * UNITS + k + 1)
                    if k >= 2:
                        dve.wait_ge(hc_ready, b * UNITS + k - 1)
                    for r in range(B):
                        part_t = slice(r * S, r * S + S)
                        last = dve.tensor_tensor_scan(hs[:, k % 2, part_t], dA[:, k % SLOTS, part_t],
                                                      dBu[:, k % SLOTS, part_t], 0.0, ALU.mult, ALU.add)
                    last.then_inc(scanned, 1)

                def times_c(k):
                    state = k // NC
                    dve.wait_ge(c_loaded[state % 2], b * (NPB // 2 * 16) + 16 * (state // 2 + 1))
                    dve.wait_ge(scanned, b * UNITS + SLOTS + k + 1)
                    dve.wait_ge(y_added, b * UNITS + k + 1)
                    dve.tensor_tensor(hc[:, k % SLOTS, :], hs[:, k % 2, :], cbc[:, state % 2, :], ALU.mult)\
                       .then_inc(hc_ready, 1)

                def hidden(i):
                    m, s = chunk(i), i % 2
                    dve.wait_ge(gate_act, b * (2 * NI) + 2 * i + 2)
                    step_ins = dve.scalar_tensor_tensor(ga[0:m, s, :], th[0:m, s, :], 1.0, ga[0:m, s, :], ALU.add, ALU.mult)
                    step_ins.then_inc(ga_scaled, 1)
                    dve.wait_ge(ga_scaled, b * NI + i + 1)
                    dve.scalar_tensor_tensor(hdn[0:m, i, :], ps[0:m, 6 + s, S:2 * S], up_s[0:m, i:i + 1], ga[0:m, s, :],
                                             ALU.mult, ALU.mult).then_inc(hdn_ready, 1)

                normed(xl, b * TB, 1, xl_ready)
                scan(0)
                scan(1)
                times_c(0)
                dve.wait_ge(e_ps, b + 1)
                dve.tensor_reduce(neg_max[:, :], mm_ps, axis=AX.X, op=ALU.max, negate=True).then_inc(max_ready, 1)
                scan(2)
                times_c(1)
                dve.wait_ge(exp_ready, b * TB + TB)
                step(dve.reciprocal(row_inv[:, :], row_sum[:, :]))
                then()
                for m in range(TB):
                    dve.tensor_scalar(att[:, m, :], att[:, m, :], row_inv[:, m:m + 1], None, ALU.mult).then_inc(att_ready, 1)
                scan(3)
                times_c(2)
                scan(4)
                times_c(3)
                dve.wait_ge(xm_ps, b + 1)
                step(dve.scalar_tensor_tensor(tile(b * TB, TB), ps[:, 5, :], gains[:, 0:1], tile(b * TB, TB),
                                              ALU.mult, ALU.add))
                then()
                sums(b * TB, TB)
                scan(5)
                times_c(4)
                normed(xl, b * TB, b * 2 + 2, xl2_ready)
                hidden(0)
                hidden(1)
                scan(6)
                times_c(5)
                hidden(2)
                hidden(3)
                scan(7)
                times_c(6)
                hidden(4)
                hidden(5)
                times_c(7)
                dve.wait_ge(hc_ready, b * UNITS + UNITS)
                dve.wait_ge(down_ps, b + 1)
                ffn_v = ffn[:, :].rearrange("p (t d) -> p t d", d=D)
                step(dve.tensor_tensor(ffn_v, mm_ps, dsg[:, :].unsqueeze(1).to_broadcast([P, TB, D]), ALU.mult))
                then()
                dve.tensor_tensor(tile(b * TB, TB), tile(b * TB, TB), ffn[:, :], ALU.add).then_inc(x2_ready, 1)
                dve.wait_ge(x2_ready, b + 1)
                sums(b * TB, TB)
                steps.leave(B)

            dve.wait_ge(y_ready, NC)
            dve.wait_ge(iota_ready, 2)

            with dve.Fori(0, B) as b:
                steps.enter(b, 6 + TB * 34)
                normed(xl, b * TB, 1 + 2 * B, zl_ready)
                dve.wait_ge(sz_ready, b + 1)
                dve.tensor_tensor(yz, y[:, :, ds(b * S, S)], sz, ALU.mult).then_inc(yz_ready, 1)
                dve.wait_ge(yzT_ps, b + 1)
                step(dve.scalar_tensor_tensor(tile(b * TB, TB), ps[:, 4, :], gains[:, 1:2], tile(b * TB, TB),
                                              ALU.mult, ALU.add))
                then()
                sums(b * TB, TB)
                normed(xl, b * TB, b + 2 * B + 2, xn_ready)
                for s in range(TB):
                    dve.wait_ge(sim_ready, b * 2 * TB + 2 * s + 2)
                    apart()
                    for n in range(NS):
                        step(dve.max(top[:, n, :], sims[:, s, n, :]))
                    then()
                    apart()
                    for n in range(NS):
                        last = dve.max_index(topi[:, n, :], top[:, n, :], sims[:, s, n, :])
                    step(last)
                    step(dve.tensor_tensor(cand[:, :, :, :], top[:, 0:H, :].unsqueeze(3).to_broadcast([P, H, K, K]),
                                           top[:, H:NS, :].unsqueeze(2).to_broadcast([P, H, K, K]), ALU.add))
                    then()
                    apart()
                    for h in range(H):
                        step(dve.max(best[:, h, :], cand[:, h, :, :]))
                    then()
                    apart()
                    for h in range(H):
                        step(dve.max_index(pk[:, h, :], best[:, h, :], cand[:, h, :, :].rearrange("p a b -> p (a b)")))
                    step(dve.tensor_copy(topf[:, :, :], topi[:, :, :]))
                    then()
                    pk_v = pk[:, :, :].rearrange("p h k -> p (h k)")
                    dve.tensor_single_scalar(pab[:, 0, :], pk_v, 3, ALU.logical_shift_right)
                    step(dve.tensor_single_scalar(pab[:, 1, :], pk_v, K - 1, ALU.bitwise_and))
                    then()
                    step(dve.tensor_copy(pabf[:, :], pab[:, :, :].rearrange("p a n -> p (a n)")))
                    then()
                    step(dve.tensor_tensor(eq[:, :, :, :], pabf[:, :].rearrange("p (n k) -> p n k", k=K).unsqueeze(3)
                                           .to_broadcast([P, NS, K, K]),
                                           iota_f[:, :].unsqueeze(1).unsqueeze(1).to_broadcast([P, NS, K, K]), ALU.is_equal))
                    then()
                    step(dve.tensor_tensor(eq[:, :, :, :], eq[:, :, :, :],
                                           topf[:, :, :].unsqueeze(2).to_broadcast([P, NS, K, K]), ALU.mult))
                    then()
                    step(dve.tensor_reduce(picked[:, :], eq[:, :, :, :].rearrange("p n k a -> p (n k) a"), axis=AX.X, op=ALU.add))
                    then()
                    step(dve.tensor_scalar(over[:, :], picked[:, 0:HK], float(ROWS), float(NK - 1), ALU.is_ge, ALU.mult))
                    step(dve.tensor_scalar(V[:, 0, :], picked[:, 0:HK], float(ROWS - 1), None, ALU.min))
                    then()
                    step(dve.tensor_tensor(V[:, 1, :], picked[:, HK:2 * HK], over[:, :], ALU.max))
                    step(dve.tensor_scalar(rest[:, :], best[:, :, :].rearrange("p h k -> p (h k)"), 0.0, None, ALU.max))
                    then()
                    dve.tensor_copy(part[:, :], rest[:, :]).then_inc(w_part, 1)
                    dve.wait_ge(w_part, b * (TB * 6) + s * 6 + 1)
                    dve.tensor_copy(V[:, 2, :], part[:, :]).then_inc(w_part, 1)
                    step(dve.tensor_tensor(rest[:, :], rest[:, :], part[:, :], ALU.subtract))
                    then()
                    dve.tensor_copy(part[:, :], rest[:, :]).then_inc(w_part, 1)
                    dve.wait_ge(w_part, b * (TB * 6) + s * 6 + 3)
                    dve.tensor_copy(V[:, 3, :], part[:, :]).then_inc(w_part, 1)
                    step(dve.tensor_tensor(rest[:, :], rest[:, :], part[:, :], ALU.subtract))
                    then()
                    dve.tensor_copy(part[:, :], rest[:, :]).then_inc(w_part, 1)
                    dve.wait_ge(w_part, b * (TB * 6) + s * 6 + 5)
                    dve.tensor_copy(V[:, 4, :], part[:, :]).then_inc(w_part, 1)
                    dve.wait_ge(w_part, b * (TB * 6) + s * 6 + 6)
                    step(dve.transpose(VT[:, :, :].rearrange("p q n -> p (q n)"), V[:, :, :].rearrange("p q n -> p (q n)")))
                    then()
                    step(dve.tensor_copy(VTb[:, :, :], VT[:, :, :]))
                    then()
                    step(dve.tensor_tensor(onehot1[:, :, :], iota_b[:, 0:ROWS].unsqueeze(1).to_broadcast([P, HK, ROWS]),
                                           VTb[:, 0, :].unsqueeze(2).to_broadcast([P, HK, ROWS]), ALU.is_equal))
                    step(dve.tensor_tensor(Y[:, s], iota_b[:, :].unsqueeze(1).to_broadcast([P, HK, NK]),
                                           VTb[:, 1, :].unsqueeze(2).to_broadcast([P, HK, NK]), ALU.is_equal))
                    then()
                    for q in range(PARTS):
                        last = dve.tensor_tensor(XW[:, s, q], onehot1[:, :, :],
                                                 VTb[:, 2 + q, :].unsqueeze(2).to_broadcast([P, HK, ROWS]), ALU.mult)
                    last.then_inc(xy_ready, 1)
                for s in range(TB):
                    dve.wait_ge(g_ready, b * (ROWS // 2) + ROWS // 2)
                    dve.wait_ge(w_ps, b * TB + s + 1)
                    if s:
                        dve.wait_ge(up_ps, b * TB + s)
                    dve.tensor_tensor(GW, GT[:, :, s * P:s * P + P], W_ps.rearrange("p t r -> p r t"), ALU.mult)\
                       .then_inc(gw_ready, 1)
                for s in range(TB):
                    dve.wait_ge(up_ps, b * TB + s + 1)
                    dve.wait_ge(stored, b * 16 + 1)
                    dve.scalar_tensor_tensor(fin[:, s, :], out_ps[s], gains[:, 3:4], tile(b * TB + s),
                                             ALU.mult, ALU.add).then_inc(fin_ready, 1)
                steps.leave(B)

        @block.tensor
        def _(pe):
            def turn(dst, src, signal):
                for i in range(2):
                    for j in range(2):
                        last = pe.transpose(dst[:, j, i * P:i * P + P], src[:, i, j * P:j * P + P], ident[:, :])
                last.then_inc(signal, 1)

            pe.wait_ge(ld_front, 32)
            for n in range(2 * NC):
                c, h = n // 2, n % 2
                pe.matmul(front_ps[:, c, h * 512:h * 512 + 512], in_w[:, c * P:c * P + P], ctxT[:, h * 512:h * 512 + 512],
                          start=True, stop=True).then_inc(in_ps, 1)
            pe.wait_ge(ld_small, 16 * 11)
            pe.wait_ge(u_ready, NC)
            for h in range(T // 512):
                for c in range(NC):
                    last = pe.matmul(ps[0:XD, 4 + h, :], xp_w[:, c, :], u[:, c, h * 512:h * 512 + 512],
                                     start=(c == 0), stop=(c == NC - 1))
                last.then_inc(xd_ps, 1)
            for n in range(2 * NC):
                c, h = n // 2, n % 2
                pe.wait_ge(xd_ready, 2)
                pe.wait_ge(xpad_ready, 2 * NC)
                pe.matmul(front_ps[:, c, h * 512:h * 512 + 512], dt_w[:, c * P:c * P + P], xdbl[0:DR, h * 512:h * 512 + 512],
                          start=True, stop=True).then_inc(dt_ps, 1)
            pe.wait_ge(consts_ready, 1)
            pe.wait_ge(ld_attn, 64)
            pe.wait_ge(ld_ffn, 64)
            pe.wait_ge(spv_ready, NC)
            pe.wait_ge(d_ready, NC)
            for c in range(NC):
                for h in range(2):
                    pe.matmul(y_ps[:, c, h * 512:h * 512 + 512], ident_d[:, c, :], u[:, c, h * 512:h * 512 + 512],
                              start=True, stop=False, skip_group_check=True)
            pe.sem_inc(y_added, SLOTS)

            with pe.Fori(0, B) as b:
                def add_y(k):
                    c = k % NC
                    pe.wait_ge(hc_ready, b * UNITS + k + 1)
                    for h in range(2):
                        last = pe.matmul(y_ps[:, c, h * 512:h * 512 + 512], ident[:, :], hc[:, k % SLOTS, h * 512:h * 512 + 512],
                                         start=False, stop=False, skip_group_check=True)
                    last.then_inc(y_added, 1)

                def gate_up(i):
                    m, s = chunk(i), i % 2
                    if i >= 2:
                        pe.wait_ge(hdn_ready, b * NI + i - 1)
                    for n, w in enumerate((gate_w, up_w)):
                        for k in range(DK_F):
                            last = pe.matmul(ps[0:m, 6 + s, n * S:n * S + S], w[:, k, i * P:i * P + m], xlT[:, k, :],
                                             start=(k == 0), stop=(k == DK_F - 1))
                    last.then_inc(gu_ps, 1)

                pe.wait_ge(xl_ready, b * TB + TB)
                turn(T_ps, xl, xlT_ps)
                pe.matmul(mm_ps[:, 0, :], wqT[:, :], ctxT[:, ds(b * S, S)], start=True, stop=True)
                pe.matmul(mm_ps[:, 1, :], wkT[:, :], ctxT[:, ds(b * S, S)], start=True, stop=True).then_inc(qk_ps, 1)
                pe.wait_ge(qk_ready, b * 2 + 2)
                for m in range(TB):
                    last = pe.matmul(mm_ps[:, m, :], qT[:, m * P:m * P + P], kT[:, :], start=True, stop=True)
                last.then_inc(e_ps, 1)
                add_y(0)
                add_y(1)
                pe.wait_ge(att_ready, b * TB + TB)
                pe.wait_ge(xlT_ready, b + 1)
                turn(T_ps, att, attT_ps)
                pe.wait_ge(attT_ready, b + 1)
                for l in range(TB):
                    for k in range(TB):
                        last = pe.matmul(mm_ps[:, l, :], xlT[:, k, l * P:l * P + P], attT[:, k, :],
                                         start=(k == 0), stop=(k == TB - 1))
                last.then_inc(xm_ps, 1)
                add_y(2)
                add_y(3)
                add_y(4)
                pe.wait_ge(xl2_ready, b * TB + TB)
                turn(T_ps, xl, xl2T_ps)
                pe.wait_ge(xl2T_ready, b + 1)
                for i in range(4):
                    gate_up(i)
                add_y(5)
                gate_up(4)
                gate_up(5)
                add_y(6)
                pe.wait_ge(hdn_ready, b * NI + NI)
                for t in range(TB):
                    for i in range(NI):
                        m = chunk(i)
                        last = pe.matmul(mm_ps[:, t, :], hdn[0:m, i, t * P:t * P + P], down_w[0:m, i, :],
                                         start=(i == 0), stop=(i == NI - 1))
                last.then_inc(down_ps, 1)
                add_y(7)

            pe.wait_ge(ld_keys, 32)
            pe.wait_ge(ld_exp, 32)
            pe.wait_ge(y_ready, NC)
            with pe.Fori(0, B) as b:
                pe.wait_ge(yz_ready, b + 1)
                turn(T_ps, yz, yzT_ps)
                pe.wait_ge(xn_ready, b * TB + TB)
                turn(T_ps, xl, xnT_ps)
                pe.wait_ge(xnT_ready, b + 1)
                for n in range(2):
                    for h in range(2 * n, 2 * n + 2):
                        for k in range(DK_F):
                            last = pe.matmul(ps[:, 5 + n, (h % 2) * S:(h % 2) * S + S], wqp[:, k, h * P:h * P + P], xnT[:, k, :],
                                             start=(k == 0), stop=(k == DK_F - 1))
                    last.then_inc(q_ps, 1)
                pe.wait_ge(q_ready, b * 2 + 2)
                for s in range(TB):
                    for side in range(2):
                        if s:
                            pe.wait_ge(sim_ready, b * 2 * TB + side + 1)
                        half = slice(side * DK, side * DK + DK)
                        for h in range(H):
                            last = pe.matmul(ps[:, 5 + side, h * NK:h * NK + NK], qTp[half, h, s * P:s * P + P],
                                             keysT[half, h, :], start=True, stop=True)
                        last.then_inc(sim_ps, 1)
                for n in range(ROWS // 2):
                    if n < 2:
                        pe.wait_ge(sim_ready, b * 2 * TB + 2 * TB - 1 + n)
                    else:
                        pe.wait_ge(g_ready, b * (ROWS // 2) + n - 1)
                    for r in range(2):
                        row = 2 * n + r
                        for k in range(DK_F):
                            last = pe.matmul(ps[:, 5 + n % 2, r * S:r * S + S], e_down[:, k, row * NK:row * NK + NK], xnT[:, k, :],
                                             start=(k == 0), stop=(k == DK_F - 1))
                    last.then_inc(g_ps, 1)
                for s in range(TB):
                    pe.wait_ge(xy_ready, b * TB + s + 1)
                    if s:
                        pe.wait_ge(gw_ready, b * TB + s)
                    for j in range(HK):
                        for q in range(PARTS):
                            for g in range(P // HK):
                                rows = slice(g * HK, g * HK + HK)
                                last = pe.matmul(W_ps[:, g * HK + j, :], Y[rows, s, j, :], XW[rows, s, q, j, :],
                                                 start=(q == 0), stop=(q == PARTS - 1), skip_group_check=True)
                    last.then_inc(w_ps, 1)
                    pe.wait_ge(gw_ready, b * TB + s + 1)
                    for r in range(ROWS):
                        last = pe.matmul(out_ps[s], GW[:, r, :], e_up[:, r, :], start=(r == 0), stop=(r == ROWS - 1))
                    last.then_inc(up_ps, 1)


def columns(v, n):
    full = np.zeros((n * P,), v.dtype)
    full[:v.size] = v.reshape(-1)
    return np.ascontiguousarray(full.reshape(n, P).T)


def kernel(**inputs):
    import concourse.bacc as bacc
    from concourse.bass_utils import run_bass_kernel_spmd

    a = {k: np.asarray(v) for k, v in inputs.items()}
    t = lambda m: np.ascontiguousarray(m.T)
    arrays = {
        "x": np.ascontiguousarray(a["x"].reshape(T, D)),
        "ctxT": t(a["ctx_1024"].reshape(T, CTX)),
        "gates": np.concatenate([a["g_xattn"], a["g_ffn"]]).reshape(1, 4),
        "wqT": t(a["L0_xattn_Wq"]), "wkT": t(a["L0_xattn_Wk"]),
        "bq": a["L0_xattn_bq"].reshape(P, 1), "bk": a["L0_xattn_bk"].reshape(P, 1),
        "gate_wT": t(a["L0_ffn_gate_w"]), "up_wT": t(a["L0_ffn_up_w"]), "down_wT": t(a["L0_ffn_down_w"]),
        "gate_s": columns(a["L0_ffn_gate_s"], NI), "up_s": columns(a["L0_ffn_up_s"], NI),
        "down_s": a["L0_ffn_down_s"].reshape(1, D),
        "in_wT": t(a["L1_xattn_in_proj_w"]), "conv_w": a["L1_xattn_conv_w"],
        "conv_b": columns(a["L1_xattn_conv_b"], NC),
        "xp_wT": t(a["L1_xattn_x_proj_w"]), "dt_wT": t(a["L1_xattn_dt_proj_w"]),
        "dt_b": columns(a["L1_xattn_dt_proj_b"], NC), "A_log": a["L1_xattn_A_log"],
        "D": columns(a["L1_xattn_D"], NC),
        "wqp": a["L1_ffn_Wq"],
        "keysT": np.ascontiguousarray(a["L1_ffn_keys"].transpose(2, 3, 0, 1).reshape(2 * DK, H * NK)),
        "e_downT": t(a["L1_ffn_e_down"]), "e_up": a["L1_ffn_e_up"],
    }
    arrays = {k: np.ascontiguousarray(v) for k, v in arrays.items()}
    nc = bacc.Bacc("TRN2", target_bir_lowering=False, num_devices=1)
    io = {k: nc.dram_tensor(k, v.shape, mybir.dt.float32, kind="ExternalInput").ap() for k, v in arrays.items()}
    out = nc.dram_tensor("out", (T, D), mybir.dt.float32, kind="ExternalOutput").ap()
    build(nc, io, out)
    got = run_bass_kernel_spmd(nc, [arrays], core_ids=[0]).results[0]["out"]
    return np.asarray(got).reshape(B, S, D)
```

```python
import numpy as np
import concourse.bass as bass
from concourse import mybir
from contextlib import ExitStack

P = 128
B, S, D = 4, 256, 256
CTX = 128
T = B * S
NT = T // P
TB = S // P
DK_F = D // P
INTER = 704
NI = (INTER + P - 1) // P
LAST = INTER - (NI - 1) * P
DI, DS, DC, DR = 256, 16, 4, 8
NC = DI // P
XD = DR + 2 * DS
H, K, DK, NK, E = 4, 8, 64, 128, 2048
ROWS = E // NK
HK = H * K
EPS = 1e-5
NPB = DS // B
UNITS = NPB * NC
SLOTS = 4
PAD = S + DC - 1
GATE_BANKS = (4, 7, 0, 1)
GROUPS = P // HK
PARTS = 3


def build(nc, io, out):
    f32, b16, u32, i32 = mybir.dt.float32, mybir.dt.bfloat16, mybir.dt.uint32, mybir.dt.int32
    ALU, ACT, AX = mybir.AluOpType, mybir.ActivationFunctionType, mybir.AxisListType
    ds = bass.ds
    ctx = ExitStack()
    with ctx:
        def sb(name, shape, dt=f32):
            return ctx.enter_context(nc.sbuf_tensor("sb_" + name, shape, dt))

        def sem(name):
            return ctx.enter_context(nc.semaphore(name))

        x = sb("x", [P, NT * D])
        ctxT = sb("ctxT", [P, T])
        wqT, wkT = sb("wqT", [P, P]), sb("wkT", [P, P])
        bq, bk = sb("bq", [P, 1]), sb("bk", [P, 1])
        gate_w, up_w = sb("gate_w", [P, DK_F, INTER]), sb("up_w", [P, DK_F, INTER])
        down_w = sb("down_w", [P, NI, D])
        gate_s, up_s, half_gs = sb("gate_s", [P, NI]), sb("up_s", [P, NI]), sb("half_gs", [P, NI])
        down_s, dsg = sb("down_s", [P, D]), sb("dsg", [P, D])
        in_w = sb("in_w", [P, DI])
        conv_w, conv_b = sb("conv_w", [P, NC, DC]), sb("conv_b", [P, NC])
        xp_w = sb("xp_w", [P, NC, XD])
        dt_w, dt_b = sb("dt_w", [DR, DI]), sb("dt_b", [P, NC])
        A = sb("A", [P, NC * DS])
        Dp = sb("Dp", [P, NC])
        wqp = sb("wqp", [P, DK_F, H * P])
        keysT = sb("keysT", [P, H, NK])
        e_down = sb("e_down", [P, DK_F, E])
        e_up = sb("e_up", [P, ROWS, D])
        gains = sb("gains", [P, 4])
        ident = sb("ident", [P, P])
        ident_d = sb("ident_d", [P, NC, P])
        iota_i = sb("iota_i", [P, P], i32)
        iota_f = sb("iota_f", [P, P])
        group = sb("group", [P, GROUPS, HK], b16)
        minus_half = sb("minus_half", [P, NT])
        stats = sb("stats", [P, NT, 6])
        mv = sb("mv", [P, NT, 2])
        mean = sb("mean", [P, NT])
        veps, rstd = sb("veps", [P, NT]), sb("rstd", [P, NT])
        xl = sb("xl", [P, TB, D])
        xlT = sb("xlT", [P, DK_F, S])
        qT, kT = sb("qT", [P, S]), sb("kT", [P, S])
        neg_max, row_sum, row_inv = sb("neg_max", [P, TB]), sb("row_sum", [P, TB]), sb("row_inv", [P, TB])
        att = sb("att", [P, TB, S])
        attT = sb("attT", [P, TB, S])
        th = sb("th", [P, 2, S])
        ga = sb("ga", [P, 2, S])
        x2T = sb("x2T", [P, DK_F, S])
        hdn = sb("hdn", [P, NI, S])
        ffn = sb("ffn", [P, TB * D])
        u = sb("u", [P, NC, T])
        delta = sb("delta", [P, NC, T])
        du = sb("du", [P, NC, T])
        xdbl = sb("xdbl", [XD, T])
        arena = sb("arena", [P, 18 * T])
        xpad = arena[:, 0:NC * B * PAD].rearrange("p (c b s) -> p c b s", c=NC, b=B)
        conv = arena[:, 3 * T:5 * T].rearrange("p (c b s) -> p c b s", c=NC, b=B)
        sp_v = arena[:, 5 * T:7 * T].rearrange("p (c t) -> p c t", c=NC)
        sp_e = arena[:, 7 * T:9 * T].rearrange("p (c t) -> p c t", c=NC)
        sp_w = arena[:, 9 * T:11 * T].rearrange("p (c t) -> p c t", c=NC)
        sp_l = arena[:, 11 * T:13 * T].rearrange("p (c t) -> p c t", c=NC)
        sp_i = arena[:, 13 * T:15 * T].rearrange("p (c t) -> p c t", c=NC)
        dA = arena[:, 0:4 * T].rearrange("p (s t) -> p s t", s=SLOTS)
        dBu = arena[:, 4 * T:8 * T].rearrange("p (s t) -> p s t", s=SLOTS)
        hs = arena[:, 8 * T:10 * T].rearrange("p (s t) -> p s t", s=2)
        hc = arena[:, 10 * T:14 * T].rearrange("p (s t) -> p s t", s=SLOTS)
        bbc = arena[:, 14 * T:16 * T].rearrange("p (s t) -> p s t", s=2)
        cbc = arena[:, 16 * T:18 * T].rearrange("p (s t) -> p s t", s=2)
        GT = arena[:, 0:4 * T].rearrange("p (r t) -> p r t", r=ROWS)
        Y = arena[:, 4 * T:8 * T].bitcast(b16).rearrange("p (s k j) -> p s k j", s=TB, k=NK)
        XW = arena[:, 8 * T:14 * T].bitcast(b16).rearrange("p (s q g r j) -> p s q g r j", s=TB, q=PARTS, g=GROUPS, r=ROWS)
        iota_k = arena[:, 16 * T:18 * T].bitcast(b16).rearrange("p (k j) -> p k j", k=NK)
        sims = du[:, :, :].rearrange("p c t -> p (c t)").rearrange("p (s n k) -> p s n k", s=TB, k=NK)
        xnT = arena[:, 14 * T:14 * T + DK_F * S].rearrange("p (k t) -> p k t", k=DK_F)
        qTp = arena[:, 15 * T:16 * T].rearrange("p (h t) -> p h t", h=H)
        gated = u
        spare = delta[:, :, :].rearrange("p c t -> p (c t)")
        fin = spare[:, 0:TB * D].rearrange("p (s d) -> p s d", s=TB)
        onehot1 = spare[:, T:T + HK * ROWS // 2].bitcast(b16).rearrange("p (r j) -> p r j", r=ROWS)
        NS = 2 * H
        top = sb("top", [P, NS, K])
        topi = sb("topi", [P, NS, K], u32)
        topf = sb("topf", [P, NS, K])
        cand = sb("cand", [P, H, K, K])
        best = sb("best", [P, H, K])
        pk = sb("pk", [P, H, K], u32)
        pab = sb("pab", [P, 2, HK], u32)
        pabf = sb("pabf", [P, 2 * HK])
        eq = sb("eq", [P, NS, K, K])
        picked = sb("picked", [P, 2 * HK])
        over = sb("over", [P, HK])
        V = sb("V", [P, 3, HK])
        VT = sb("VT", [P, 3, HK])
        rest = sb("rest", [P, HK])
        keys_b = sb("keys_b", [P, 2, HK], b16)
        part = sb("part", [P, PARTS, HK], b16)
        WG = sb("WG", [P, PARTS, GROUPS, HK], b16)

        ps = ctx.enter_context(nc.psum_tensor("ps", [P, 8, 512], f32))
        y_ps = ps[:, 0:4, :].rearrange("p (c h) s -> p c (h s)", c=NC)
        front_ps = y_ps
        T_ps = ps[:, 4, :].rearrange("p (k s) -> p k s", k=2)
        mm_ps = ps[:, 5, :].rearrange("p (k s) -> p k s", k=2)
        down_ps_v = ps[:, 6, :].rearrange("p (k s) -> p k s", k=2)
        out_ps = [ps[:, 7, 0:D], ps[:, 4, 0:D]]
        W_ps = ps[:, 0:4, :].rearrange("p b (j g r) -> p (b j) g r", g=GROUPS, r=ROWS)

        scratch = nc.dram_tensor("bc_scratch", [2 * DS, T], f32, kind="Internal").ap()

        ld_x, ld_front, ld_small, ld_attn, ld_ffn = (sem("ld_" + n) for n in ("x", "front", "small", "attn", "ffn"))
        ld_keys, ld_exp = sem("ld_keys"), sem("ld_exp")
        consts_ready, iota_ready, pads_ready = sem("consts_ready"), sem("iota_ready"), sem("pads_ready")
        act_step, pool_step = sem("act_step"), sem("pool_step")
        front_step, attn_step, feed_step, keys_step = (sem(n + "_step") for n in ("front", "attn", "feed", "keys"))
        paired, ld_front2, ld_small2 = sem("paired"), sem("ld_front2"), sem("ld_small2")
        ga_scaled, d_ready, top_step = sem("ga_scaled"), sem("d_ready"), sem("top_step")
        iota_k_ready = sem("iota_k_ready")
        dve_passed, pool_passed = sem("dve_passed"), sem("pool_passed")
        veps_ready, rstd_ready = sem("veps_ready"), sem("rstd_ready")
        gains_ready = sem("gains_ready")
        in_ps, xpad_ready, conv_ready, u_ready = sem("in_ps"), sem("xpad_ready"), sem("conv_ready"), sem("u_ready")
        xd_ps, xd_ready, xd_stored, dt_ps = sem("xd_ps"), sem("xd_ready"), sem("xd_stored"), sem("dt_ps")
        spv_ready, spe_ready, spw_ready = sem("spv_ready"), sem("spe_ready"), sem("spw_ready")
        spl_ready, spi_ready, a_ready = sem("spl_ready"), sem("spi_ready"), sem("a_ready")
        delta_ready, du_ready = sem("delta_ready"), sem("du_ready")
        b_loaded = [sem("b_loaded0"), sem("b_loaded1")]
        c_loaded = [sem("c_loaded0"), sem("c_loaded1")]
        da_ready, dbu_ready, scanned, hc_ready, y_added = (sem(n) for n in (
            "da_ready", "dbu_ready", "scanned", "hc_ready", "y_added"))
        xl_ready, xlT_ps, xlT_ready = sem("xl_ready"), sem("xlT_ps"), sem("xlT_ready")
        qk_ps, qk_ready, e_ps, max_ready, exp_ready = (sem(n) for n in (
            "qk_ps", "qk_ready", "e_ps", "max_ready", "exp_ready"))
        att_ready, attT_ps, attT_ready, xm_ps = (sem(n) for n in ("att_ready", "attT_ps", "attT_ready", "xm_ps"))
        xl2_ready, xl2T_ps, xl2T_ready = sem("xl2_ready"), sem("xl2T_ps"), sem("xl2T_ready")
        gu_ps, gate_act, hdn_ready, down_ps, x2_ready = (sem(n) for n in (
            "gu_ps", "gate_act", "hdn_ready", "down_ps", "x2_ready"))
        zl_ready, sz_ready, yz_ready, yzT_ps = (sem(n) for n in ("zl_ready", "sz_ready", "yz_ready", "yzT_ps"))
        xn_ready, xnT_ps, xnT_ready = sem("xn_ready"), sem("xnT_ps"), sem("xnT_ready")
        q_ps, q_ready, sim_ps, sim_ready, g_ps, g_ready = (sem(n) for n in (
            "q_ps", "q_ready", "sim_ps", "sim_ready", "g_ps", "g_ready"))
        xw_ready, w_ps, gw_ready, up_ps, fin_ready, stored = (sem(n) for n in (
            "xw_ready", "w_ps", "gw_ready", "up_ps", "fin_ready", "stored"))

        block = ctx.enter_context(nc.Block())

        class Steps:

            def __init__(self, per=0):
                self.per, self.base, self.inner = per, 0, 0

            def begin(self, i):
                self.base, self.inner = i * self.per, 0

            def one(self):
                self.inner += 1
                return 1

            def now(self):
                return self.base + self.inner

            def end(self):
                assert self.inner == self.per, (self.inner, self.per)

        def chunk(i):
            return P if i < NI - 1 else LAST


        @block.sync
        def _(sp):
            sp.dma_start(ctxT[:, 0:T // 2], io["ctxT"][:, 0:T // 2]).then_inc(ld_front, 16)
            sp.dma_start(in_w[:, :], io["in_wT"]).then_inc(ld_front, 16)
            sp.dma_start(ctxT[:, T // 2:T], io["ctxT"][:, T // 2:T]).then_inc(ld_front2, 16)
            sp.dma_start(x[:, :].rearrange("p (t d) -> p t d", d=D),
                         io["x"].rearrange("(t p) d -> p t d", p=P)).then_inc(ld_x, 16)
            sp.dma_start(wqT[:, :], io["wqT"]).then_inc(ld_attn, 16)
            sp.dma_start(wkT[:, :], io["wkT"]).then_inc(ld_attn, 16)
            sp.dma_start(bq[:, :], io["bq"]).then_inc(ld_attn, 16)
            sp.dma_start(bk[:, :], io["bk"]).then_inc(ld_attn, 16)
            sp.dma_start(gate_w[:, :, :], io["gate_wT"].rearrange("(k p) n -> p k n", p=P)).then_inc(ld_ffn, 16)
            sp.dma_start(up_w[:, :, :], io["up_wT"].rearrange("(k p) n -> p k n", p=P)).then_inc(ld_ffn, 16)
            full = (NI - 1) * P
            sp.dma_start(down_w[:, 0:NI - 1, :], io["down_wT"][0:full, :].rearrange("(k p) n -> p k n", p=P)).then_inc(ld_ffn, 16)
            sp.dma_start(down_w[0:LAST, NI - 1, :], io["down_wT"][full:INTER, :]).then_inc(ld_ffn, 16)
            sp.wait_ge(xd_ready, T // 512)
            sp.dma_start(scratch, xdbl[DR:XD, :]).then_inc(xd_stored, 16)
            sp.wait_ge(xd_stored, 16)

            def spread_b(row, slot):
                sp.dma_start(bbc[:, slot, :], scratch[row, :].broadcast_to([P, T])).then_inc(b_loaded[slot], 16)

            def spread_c(row, slot):
                sp.dma_start(cbc[:, slot, :], scratch[row, :].broadcast_to([P, T])).then_inc(c_loaded[slot], 16)

            sp.wait_ge(delta_ready, NC)
            for slot in range(2):
                spread_b(slice(slot, slot + 1), slot)
                spread_c(slice(DS + slot, DS + slot + 1), slot)
            with sp.Fori(0, DS // 2 - 1) as m:
                for slot in range(2):
                    sp.wait_ge(dbu_ready, m * (2 * NC) + NC * (slot + 1))
                    spread_b(ds(m * 2 + 2 + slot, 1), slot)
                    sp.wait_ge(hc_ready, m * (2 * NC) + NC * (slot + 1))
                    spread_c(ds(m * 2 + 2 + slot + DS, 1), slot)
            sp.sem_inc(stored, 1)
            with sp.Fori(0, B) as b:
                for s in range(TB):
                    sp.wait_ge(fin_ready, b * TB + s + 1)
                    sp.dma_start(out.rearrange("(t p) d -> p t d", p=P)[:, ds(b * TB + s, 1), :],
                                 fin[:, s:s + 1, :]).then_inc(stored, 16)
            sp.wait_ge(stored, 16 * NT + 1)

        @block.gpsimd
        def _(pool):
            pool.memset(xpad[:, :, :, 0:DC - 1], 0.0).then_inc(pads_ready, 1)
            pool.memset(minus_half[:, :], -0.5).then_inc(pool_step, 1)
            pool.memset(ident[:, :], 0.0).then_inc(pool_step, 1)
            pool.wait_ge(pool_step, 2)
            pool.affine_select(out=ident[:, :], in_=ident[:, :], compare_op=ALU.not_equal, fill=1.0,
                               base=0, pattern=[[-1, P]], channel_multiplier=1).then_inc(consts_ready, 1)
            pool.iota(iota_i[:, :], pattern=[[1, P]], base=0, channel_multiplier=0).then_inc(pool_step, 1)
            pool.wait_ge(pool_step, 3)
            pool.tensor_copy(iota_f[:, :], iota_i[:, :]).then_inc(iota_ready, 1)
            pool.memset(group[:, :, :], 0.0).then_inc(pool_step, 1)
            pool.wait_ge(pool_step, 4)
            for g in range(GROUPS):
                pool.memset(group[g * HK:g * HK + HK, g, :], 1.0).then_inc(iota_ready, 1)
            pool.wait_ge(iota_ready, 1 + GROUPS)

            def power(first, tiles, n):
                pool.wait_ge(veps_ready, n)
                pool.sem_inc(pool_passed, 1)
                pool.tensor_tensor(rstd[:, ds(first, tiles)], veps[:, ds(first, tiles)], minus_half[:, 0:tiles], ALU.pow)\
                    .then_inc(rstd_ready, 1)

            def times_b(b, k):
                state, c = k // NC, k % NC
                pool.wait_ge(b_loaded[state % 2], b * (NPB // 2 * 16) + 16 * (state // 2 + 1))
                pool.wait_ge(scanned, b * UNITS + k + 1)
                pool.tensor_tensor(dBu[:, k % SLOTS, :], du[:, c, :], bbc[:, state % 2, :], ALU.mult)\
                    .then_inc(dbu_ready, 1)

            def add_pair(b, j):
                k = (j // 2) * SLOTS + j % 2
                pool.wait_ge(hc_ready, b * UNITS + k + NC + 1)
                pool.tensor_tensor(hc[:, k % SLOTS, :], hc[:, k % SLOTS, :], hc[:, (k + NC) % SLOTS, :], ALU.add)\
                    .then_inc(paired, 1)

            power(0, NT, 1)
            pool.wait_ge(rstd_ready, 1)
            pool.wait_ge(du_ready, NC)
            pool.dma_start(wqp[:, :, :], io["wqp"].rearrange("(k p) n -> p k n", p=P)).then_inc(ld_keys, 16)
            pool.dma_start(keysT[:, :, :], io["keysT"].rearrange("p (h k) -> p h k", h=H)).then_inc(ld_keys, 16)
            pool.dma_start(e_down[:, :, :], io["e_downT"].rearrange("(k p) n -> p k n", p=P)).then_inc(ld_exp, 16)
            pool.dma_start(e_up[:, :, :], io["e_up"].rearrange("(r p) n -> p r n", p=P)).then_inc(ld_exp, 16)
            power(0, TB, 2)

            def merged(b, more):
                times_b(b, 0)
                times_b(b, 1)
                times_b(b, 2)
                times_b(b, 3)
                times_b(b, 4)
                add_pair(b, 0)
                times_b(b, 5)
                add_pair(b, 1)
                times_b(b, 6)
                times_b(b, 7)
                add_pair(b, 2)
                if more:
                    power((b + 1) * TB, TB, b * 2 + 3)
                add_pair(b, 3)
                power(b * TB, TB, b * 2 + (4 if more else 3))

            with pool.Fori(0, B - 1) as b:
                merged(b, True)
            merged(B - 1, False)

            power(0, TB, 2 * B + 2)
            power(TB, NT - TB, 2 * B + 3)

        @block.scalar
        def _(act):
            act.dma_start(conv_w[:, :, :], io["conv_w"].rearrange("(c p) n -> p c n", p=P)).then_inc(ld_small, 16)
            act.dma_start(conv_b[:, :], io["conv_b"]).then_inc(ld_small, 16)
            act.dma_start(xp_w[:, :, :], io["xp_wT"].rearrange("(c p) n -> p c n", p=P)).then_inc(ld_small2, 16)
            act.dma_start(dt_w[:, :], io["dt_wT"]).then_inc(ld_small2, 16)
            for dst, name in ((dt_b, "dt_b"), (Dp, "D")):
                act.dma_start(dst[:, :], io[name]).then_inc(ld_small2, 16)
            act.dma_start(A[:, :].rearrange("p (c n) -> p c n", c=NC),
                          io["A_log"].rearrange("(c p) n -> p c n", p=P)).then_inc(ld_small2, 16)
            act.dma_start(gains[:, :], io["gates"].broadcast_to([P, 4])).then_inc(ld_small2, 16)
            act.dma_start(gate_s[:, :], io["gate_s"]).then_inc(ld_small2, 16)
            act.dma_start(up_s[:, :], io["up_s"]).then_inc(ld_small2, 16)
            act.dma_start(down_s[:, :], io["down_s"].broadcast_to([P, D])).then_inc(ld_small2, 16)

            act.wait_ge(pads_ready, 1)
            for n in range(2 * NC):
                c, h = n // 2, n % 2
                act.wait_ge(in_ps, n + 1)
                act.copy(xpad[:, c, 2 * h:2 * h + 2, DC - 1:PAD],
                         front_ps[:, c, h * 512:h * 512 + 512].rearrange("p (b s) -> p b s", b=2)).then_inc(xpad_ready, 1)
            act.wait_ge(ld_small, 32)
            for c in range(NC):
                act.wait_ge(conv_ready, c + 1)
                act.activation(u[:, c, :].rearrange("p (b s) -> p b s", b=B), conv[:, c], ACT.Silu,
                               bias=conv_b[:, c:c + 1]).then_inc(u_ready, 1)
            act.wait_ge(ld_small2, 16 * 9)
            act.activation(gains[:, :], gains[:, :], ACT.Tanh).then_inc(gains_ready, 1)
            act.activation(A[:, :], A[:, :], ACT.Exp).then_inc(act_step, 1)
            for h in range(T // 512):
                act.wait_ge(xd_ps, h + 1)
                act.copy(xdbl[:, h * 512:h * 512 + 512], ps[0:XD, 4 + h, :]).then_inc(xd_ready, 1)
            act.wait_ge(act_step, 1)
            act.mul(A[:, :], A[:, :], -1.0).then_inc(a_ready, 1)
            for c in range(NC):
                act.wait_ge(dt_ps, 2 * (c + 1))
                act.activation(sp_v[:, c, :], front_ps[:, c, :], ACT.Identity, bias=dt_b[:, c:c + 1]).then_inc(spv_ready, 1)
                act.wait_ge(spv_ready, c + 1)
                act.activation(sp_e[:, c, :], sp_v[:, c, :], ACT.Abs).then_inc(act_step, 1)
                act.wait_ge(act_step, c + 2)
                act.activation(sp_e[:, c, :], sp_e[:, c, :], ACT.Exp, scale=-1.0).then_inc(spe_ready, 1)

            def copy_xlT(i):
                act.wait_ge(xlT_ps, i + 1)
                act.copy(xlT[:, :, :], T_ps).then_inc(xlT_ready, 1)

            def copy_qk(i):
                act.wait_ge(qk_ps, i + 1)
                act.activation(qT[:, :], mm_ps[:, 0, :], ACT.Identity, bias=bq[:, :]).then_inc(qk_ready, 1)
                act.activation(kT[:, :], mm_ps[:, 1, :], ACT.Identity, bias=bk[:, :]).then_inc(qk_ready, 1)

            def softmax_exp(i):
                act.wait_ge(max_ready, i + 1)
                for m in range(TB):
                    act.activation(att[:, m, :], mm_ps[:, m, :], ACT.Exp, bias=neg_max[:, m:m + 1],
                                   accum_out=row_sum[:, m:m + 1]).then_inc(exp_ready, 1)

            def copy_attT(i):
                act.wait_ge(attT_ps, i + 1)
                act.copy(attT[:, :, :], T_ps).then_inc(attT_ready, 1)

            def copy_x2T(i):
                act.wait_ge(xl2T_ps, i + 1)
                act.copy(x2T[:, :, :], T_ps).then_inc(xl2T_ready, 1)

            act.wait_ge(ld_attn, 64)
            copy_xlT(0)
            copy_qk(0)
            for c in range(NC):
                act.wait_ge(spw_ready, c + 1)
                act.activation(sp_l[:, c, :], sp_w[:, c, :], ACT.Ln).then_inc(spl_ready, 1)
            for c in range(NC):
                act.wait_ge(spl_ready, c + 1)
                act.activation(sp_i[:, c, :], sp_l[:, c, :], ACT.Exp, scale=-1.0).then_inc(spi_ready, 1)
            softmax_exp(0)
            copy_attT(0)
            copy_x2T(0)
            act.wait_ge(a_ready, 1)
            act.wait_ge(delta_ready, NC)

            def merged(b, more):
                def decay(k):
                    state, c = k // NC, k % NC
                    act.wait_ge(scanned, b * UNITS + k + 1)
                    act.activation(dA[:, k % SLOTS, :], delta[:, c, :], ACT.Exp,
                                   scale=A[:, ds(b * NPB + (c * DS + state), 1)]).then_inc(da_ready, 1)

                def gate(i):
                    m, s = chunk(i), i % 2
                    act.wait_ge(gu_ps, b * NI + i + 1)
                    if i >= 2:
                        act.wait_ge(hdn_ready, b * NI + i - 1)
                    act.activation(th[0:m, s, :], ps[0:m, 6 + s, 0:S], ACT.Tanh, scale=half_gs[0:m, i:i + 1])\
                        .then_inc(gate_act, 1)
                    act.activation(ga[0:m, s, :], ps[0:m, 6 + s, 0:S], ACT.Copy, scale=half_gs[0:m, i:i + 1])\
                        .then_inc(gate_act, 1)

                decay(0)
                decay(1)
                gate(0)
                if more:
                    copy_qk(b + 1)
                decay(2)
                gate(1)
                decay(3)
                decay(4)
                if more:
                    copy_xlT(b + 1)
                gate(2)
                decay(5)
                if more:
                    softmax_exp(b + 1)
                decay(6)
                gate(3)
                decay(7)
                gate(4)
                gate(5)
                if more:
                    copy_attT(b + 1)
                    copy_x2T(b + 1)

            with act.Fori(0, B - 1) as b:
                merged(b, True)
            merged(B - 1, False)

            for n, batches in enumerate((slice(0, (B - 1) * S), slice((B - 1) * S, B * S))):
                act.wait_ge(zl_ready, (B - 1 + n) * TB)
                act.activation(gated[:, :, batches], gated[:, :, batches], ACT.Silu).then_inc(sz_ready, 1)

            act.wait_ge(y_added, B * UNITS // 2 + 2)
            act.wait_ge(iota_ready, 1 + GROUPS)
            act.copy(iota_k, iota_f[:, :].unsqueeze(2).to_broadcast([P, NK, HK])).then_inc(iota_k_ready, 1)

            def keys_in(i):
                act.wait_ge(xnT_ps, i + 1)
                act.copy(xnT, T_ps).then_inc(xnT_ready, 1)
                for n in range(2):
                    act.wait_ge(q_ps, i * 2 + n + 1)
                    act.copy(qTp[:, 2 * n:2 * n + 2, :], ps[:, 5 + n, :].rearrange("p (h t) -> p h t", h=2)).then_inc(q_ready, 1)

            def copy_sims(i, s):
                for side in range(2):
                    act.wait_ge(sim_ps, i * 2 * TB + 2 * s + side + 1)
                    act.copy(sims[:, s, side * H:side * H + H, :],
                             ps[:, 5 + side, :].rearrange("p (h k) -> p h k", h=H)).then_inc(sim_ready, 1)

            def experts(b, more):
                for n in range(ROWS // 2):
                    act.wait_ge(g_ps, b * (ROWS // 2) + n + 1)
                    act.activation(GT[:, 2 * n:2 * n + 2, :], ps[:, 5 + n % 2, :].rearrange("p (r t) -> p r t", r=2),
                                   ACT.Silu).then_inc(g_ready, 1)
                if more:
                    keys_in(b + 1)
                    copy_sims(b + 1, 0)
                    act.wait_ge(xw_ready, b * TB + TB)
                    copy_sims(b + 1, 1)

            keys_in(0)
            copy_sims(0, 0)
            copy_sims(0, 1)
            with act.Fori(0, B - 1) as b:
                experts(b, True)
            experts(B - 1, False)

        @block.vector
        def _(dve):
            front = Steps()
            attn = Steps(3 + 2 * TB)
            feed = Steps(2 + 2 * TB)
            keys = Steps()
            tops = Steps(38)

            def apart():
                dve.sem_inc(dve_passed, 1)

            def tile(i, n=1):
                return x[:, ds(i * D, n * D)]

            def sums(st, st_step, first, n):
                apart()
                for t in range(n):
                    dve.bn_stats(stats[:, t, :], tile(first + t)).then_inc(st_step, st.one())
                dve.wait_ge(st_step, st.now())
                apart()
                for t in range(n):
                    dve.bn_aggr(mv[:, t, :], stats[:, t, :]).then_inc(st_step, st.one())
                dve.wait_ge(st_step, st.now())
                apart()
                dve.tensor_copy(mean[:, ds(first, n)], mv[:, 0:n, 0]).then_inc(st_step, st.one())
                dve.tensor_scalar(veps[:, ds(first, n)], mv[:, 0:n, 1], EPS, None, ALU.add).then_inc(veps_ready, 1)

            def normed(dst, i, n_rstd, signal):
                dve.wait_ge(rstd_ready, n_rstd)
                for t in range(TB):
                    dve.tensor_scalar(dst[:, t, :], tile(i + t), mean[:, ds(i + t, 1)], rstd[:, ds(i + t, 1)],
                                      ALU.subtract, ALU.mult).then_inc(signal, 1)

            dve.wait_ge(ld_x, 16)
            sums(front, front_step, 0, NT)
            dve.wait_ge(ld_small, 32)
            for c in range(NC):
                dve.wait_ge(xpad_ready, 2 * (c + 1))
                dve.tensor_scalar(conv[:, c], xpad[:, c, :, 0:S], conv_w[:, c, 0:1], None, ALU.mult)\
                    .then_inc(front_step, front.one())
                for k in range(1, DC):
                    dve.wait_ge(front_step, front.now())
                    ins = dve.scalar_tensor_tensor(conv[:, c], xpad[:, c, :, k:k + S], conv_w[:, c, k:k + 1], conv[:, c],
                                                   ALU.mult, ALU.add)
                    if k < DC - 1:
                        ins.then_inc(front_step, front.one())
                    else:
                        ins.then_inc(conv_ready, 1)
            normed(xl, 0, 1, xl_ready)
            dve.wait_ge(ld_small2, 16 * 9)
            dve.wait_ge(consts_ready, 1)
            for c in range(NC):
                dve.tensor_scalar(ident_d[:, c, :], ident[:, :], Dp[:, c:c + 1], None, ALU.mult).then_inc(d_ready, 1)
            dve.tensor_scalar(half_gs[:, :], gate_s[:, :], 0.5, None, ALU.mult).then_inc(front_step, front.one())
            dve.wait_ge(gains_ready, 1)
            dve.tensor_scalar(dsg[:, :], down_s[:, :], gains[:, 2:3], None, ALU.mult)\
                .then_inc(front_step, front.one())
            for c in range(NC):
                dve.wait_ge(spe_ready, c + 1)
                dve.tensor_scalar(sp_w[:, c, :], sp_e[:, c, :], 1.0, None, ALU.add).then_inc(spw_ready, 1)
            for c in range(NC):
                dve.wait_ge(spw_ready, c + 1)
                dve.scalar_tensor_tensor(sp_e[:, c, :], sp_w[:, c, :], 1.0, sp_e[:, c, :], ALU.subtract, ALU.subtract)\
                    .then_inc(front_step, front.one())

            def row_max(i):
                dve.wait_ge(e_ps, i + 1)
                dve.tensor_reduce(neg_max[:, :], mm_ps, axis=AX.X, op=ALU.max, negate=True).then_inc(max_ready, 1)

            def normalise(i):
                dve.wait_ge(exp_ready, i * TB + TB)
                dve.reciprocal(row_inv[:, :], row_sum[:, :]).then_inc(attn_step, attn.one())
                dve.wait_ge(attn_step, attn.now())
                for m in range(TB):
                    dve.tensor_scalar(att[:, m, :], att[:, m, :], row_inv[:, m:m + 1], None, ALU.mult).then_inc(att_ready, 1)

            def x1(i):
                dve.wait_ge(xm_ps, i + 1)
                dve.scalar_tensor_tensor(tile(i * TB, TB), ps[:, 5, :], gains[:, 0:1], tile(i * TB, TB),
                                         ALU.mult, ALU.add).then_inc(attn_step, attn.one())
                dve.wait_ge(attn_step, attn.now())
                sums(attn, attn_step, i * TB, TB)

            row_max(0)
            for c in range(NC):
                dve.wait_ge(spi_ready, c + 1)
                dve.wait_ge(front_step, front.now())
                dve.tensor_tensor(sp_i[:, c, :], sp_e[:, c, :], sp_i[:, c, :], ALU.mult)\
                    .then_inc(front_step, front.one())
                dve.wait_ge(front_step, front.now())
                dve.tensor_tensor(sp_l[:, c, :], sp_l[:, c, :], sp_i[:, c, :], ALU.subtract)\
                    .then_inc(front_step, front.one())
                dve.wait_ge(front_step, front.now())
                dve.scalar_tensor_tensor(delta[:, c, :], sp_v[:, c, :], 0.0, sp_l[:, c, :], ALU.max, ALU.add)\
                   .then_inc(delta_ready, 1)
            for c in range(NC):
                dve.wait_ge(delta_ready, c + 1)
                dve.tensor_tensor(du[:, c, :], delta[:, c, :], u[:, c, :], ALU.mult).then_inc(du_ready, 1)
            dve.wait_ge(du_ready, NC)
            dve.sem_inc(scanned, SLOTS)
            attn.begin(0)
            normalise(0)
            x1(0)
            normed(xl, 0, 2, xl2_ready)
            attn.end()

            def merged(b, more):
                def scan(k):
                    dve.wait_ge(da_ready, b * UNITS + k + 1)
                    dve.wait_ge(dbu_ready, b * UNITS + k + 1)
                    if k >= 2:
                        dve.wait_ge(hc_ready, b * UNITS + k - 1)
                    for r in range(B):
                        part_t = slice(r * S, r * S + S)
                        last = dve.tensor_tensor_scan(hs[:, k % 2, part_t], dA[:, k % SLOTS, part_t],
                                                      dBu[:, k % SLOTS, part_t], 0.0, ALU.mult, ALU.add)
                    last.then_inc(scanned, 1)

                def times_c(k):
                    state = k // NC
                    dve.wait_ge(c_loaded[state % 2], b * (NPB // 2 * 16) + 16 * (state // 2 + 1))
                    dve.wait_ge(scanned, b * UNITS + SLOTS + k + 1)
                    dve.wait_ge(y_added, b * (UNITS // 2) + (k // SLOTS) * 2 + k % 2 + 1)
                    dve.tensor_tensor(hc[:, k % SLOTS, :], hs[:, k % 2, :], cbc[:, state % 2, :], ALU.mult)\
                       .then_inc(hc_ready, 1)

                def hidden(i):
                    m, s = chunk(i), i % 2
                    dve.wait_ge(gate_act, b * (2 * NI) + 2 * i + 2)
                    dve.scalar_tensor_tensor(ga[0:m, s, :], th[0:m, s, :], 1.0, ga[0:m, s, :], ALU.add, ALU.mult)\
                       .then_inc(ga_scaled, 1)
                    dve.wait_ge(ga_scaled, b * NI + i + 1)
                    dve.scalar_tensor_tensor(hdn[0:m, i, :], ps[0:m, 6 + s, S:2 * S], up_s[0:m, i:i + 1], ga[0:m, s, :],
                                             ALU.mult, ALU.mult).then_inc(hdn_ready, 1)

                def x2(b):
                    feed.begin(b)
                    dve.wait_ge(down_ps, b + 1)
                    dve.tensor_tensor(ffn[:, :].rearrange("p (t d) -> p t d", d=D), down_ps_v,
                                      dsg[:, :].unsqueeze(1).to_broadcast([P, TB, D]), ALU.mult)\
                        .then_inc(feed_step, feed.one())
                    dve.wait_ge(feed_step, feed.now())
                    dve.tensor_tensor(tile(b * TB, TB), tile(b * TB, TB), ffn[:, :], ALU.add).then_inc(x2_ready, 1)
                    dve.wait_ge(x2_ready, b + 1)
                    sums(feed, feed_step, b * TB, TB)
                    feed.end()

                def gate_x(b):
                    dve.wait_ge(feed_step, feed.now())
                    normed(gated[:, :, ds(b * S, S)], b * TB, b * 2 + (4 if more else 3), zl_ready)

                if more:
                    attn.begin(b + 1)
                if more:
                    dve.wait_ge(xl2T_ps, b + 1)
                    normed(xl, (b + 1) * TB, 1, xl_ready)
                scan(0)
                times_c(0)
                scan(1)
                hidden(0)
                scan(2)
                times_c(1)
                times_c(2)
                hidden(1)
                if more:
                    row_max(b + 1)
                scan(3)
                hidden(2)
                times_c(3)
                if more:
                    normalise(b + 1)
                scan(4)
                hidden(3)
                scan(5)
                times_c(4)
                scan(6)
                hidden(4)
                times_c(5)
                hidden(5)
                scan(7)
                times_c(6)
                times_c(7)
                if more:
                    x1(b + 1)
                x2(b)
                if more:
                    normed(xl, (b + 1) * TB, b * 2 + 3, xl2_ready)
                gate_x(b)
                if more:
                    attn.end()
                dve.wait_ge(hc_ready, b * UNITS + UNITS)

            with dve.Fori(0, B - 1) as b:
                merged(b, True)
            merged(B - 1, False)

            def times_y(i):
                dve.wait_ge(sz_ready, 1 if i < B - 1 else 2)
                mine = gated[:, :, i * S:i * S + S]
                dve.tensor_tensor(mine, y_ps[:, :, i * S:i * S + S], mine, ALU.mult).then_inc(yz_ready, 1)

            def x3(i):
                dve.wait_ge(yzT_ps, i + 1)
                dve.scalar_tensor_tensor(tile(i * TB, TB), ps[:, GATE_BANKS[i], :], gains[:, 1:2], tile(i * TB, TB),
                                         ALU.mult, ALU.add).then_inc(keys_step, keys.one())

            dve.wait_ge(y_added, B * UNITS // 2 + 2)
            for i in range(B):
                times_y(i)
            dve.wait_ge(zl_ready, NT)
            x3(0)
            dve.wait_ge(keys_step, keys.now())
            sums(keys, keys_step, 0, TB)
            for i in range(1, B):
                x3(i)
            normed(xl, 0, 2 * B + 2, xn_ready)
            dve.wait_ge(keys_step, keys.now())
            sums(keys, keys_step, TB, NT - TB)
            dve.wait_ge(keys_step, keys.now())

            def top_keys(i, s):
                tops.begin(i * TB + s)
                dve.wait_ge(sim_ready, i * 2 * TB + 2 * s + 2)
                apart()
                for n in range(NS):
                    dve.max(top[:, n, :], sims[:, s, n, :]).then_inc(top_step, tops.one())
                dve.wait_ge(top_step, tops.now())
                apart()
                for n in range(NS):
                    last = dve.max_index(topi[:, n, :], top[:, n, :], sims[:, s, n, :])
                last.then_inc(top_step, tops.one())
                dve.tensor_tensor(cand[:, :, :, :], top[:, 0:H, :].unsqueeze(3).to_broadcast([P, H, K, K]),
                                  top[:, H:NS, :].unsqueeze(2).to_broadcast([P, H, K, K]), ALU.add)\
                    .then_inc(top_step, tops.one())
                dve.wait_ge(top_step, tops.now())
                apart()
                for h in range(H):
                    dve.max(best[:, h, :], cand[:, h, :, :]).then_inc(top_step, tops.one())
                dve.wait_ge(top_step, tops.now())
                apart()
                for h in range(H):
                    dve.max_index(pk[:, h, :], best[:, h, :], cand[:, h, :, :].rearrange("p a b -> p (a b)"))\
                        .then_inc(top_step, tops.one())
                dve.tensor_copy(topf[:, :, :], topi[:, :, :]).then_inc(top_step, tops.one())
                dve.wait_ge(top_step, tops.now())
                pk_v = pk[:, :, :].rearrange("p h k -> p (h k)")
                dve.tensor_single_scalar(pab[:, 0, :], pk_v, 3, ALU.logical_shift_right)
                dve.tensor_single_scalar(pab[:, 1, :], pk_v, K - 1, ALU.bitwise_and).then_inc(top_step, tops.one())
                dve.wait_ge(top_step, tops.now())
                dve.tensor_copy(pabf[:, :], pab[:, :, :].rearrange("p a n -> p (a n)"))\
                    .then_inc(top_step, tops.one())
                dve.wait_ge(top_step, tops.now())
                dve.tensor_tensor(eq[:, :, :, :], pabf[:, :].rearrange("p (n k) -> p n k", k=K).unsqueeze(3)
                                  .to_broadcast([P, NS, K, K]),
                                  iota_f[:, 0:K].unsqueeze(1).unsqueeze(1).to_broadcast([P, NS, K, K]), ALU.is_equal)\
                    .then_inc(top_step, tops.one())
                dve.wait_ge(top_step, tops.now())
                dve.tensor_tensor(eq[:, :, :, :], eq[:, :, :, :],
                                  topf[:, :, :].unsqueeze(2).to_broadcast([P, NS, K, K]), ALU.mult)\
                    .then_inc(top_step, tops.one())
                dve.wait_ge(top_step, tops.now())
                dve.tensor_reduce(picked[:, :], eq[:, :, :, :].rearrange("p n k a -> p (n k) a"), axis=AX.X, op=ALU.add)\
                    .then_inc(top_step, tops.one())
                dve.wait_ge(top_step, tops.now())
                dve.tensor_scalar(over[:, :], picked[:, 0:HK], float(ROWS), float(NK - 1), ALU.is_ge, ALU.mult)\
                    .then_inc(top_step, tops.one())
                dve.tensor_scalar(V[:, 0, :], picked[:, 0:HK], float(ROWS - 1), None, ALU.min)\
                    .then_inc(top_step, tops.one())
                dve.wait_ge(top_step, tops.now())
                dve.tensor_tensor(V[:, 1, :], picked[:, HK:2 * HK], over[:, :], ALU.max)\
                    .then_inc(top_step, tops.one())
                dve.tensor_scalar(V[:, 2, :], best[:, :, :].rearrange("p h k -> p (h k)"), 0.0, None, ALU.max)\
                    .then_inc(top_step, tops.one())
                dve.wait_ge(top_step, tops.now())
                dve.transpose(VT[:, :, :].rearrange("p q n -> p (q n)"), V[:, :, :].rearrange("p q n -> p (q n)"))\
                    .then_inc(top_step, tops.one())
                dve.wait_ge(top_step, tops.now())
                dve.tensor_copy(part[:, 0, :], VT[:, 2, :]).then_inc(top_step, tops.one())
                dve.tensor_copy(keys_b[:, :, :], VT[:, 0:2, :]).then_inc(top_step, tops.one())
                dve.wait_ge(top_step, tops.now())
                dve.tensor_tensor(rest[:, :], VT[:, 2, :], part[:, 0, :], ALU.subtract).then_inc(top_step, tops.one())
                rested = tops.now()
                dve.tensor_tensor(onehot1, iota_k[:, 0:ROWS, :], keys_b[:, 0, :].unsqueeze(1).to_broadcast([P, ROWS, HK]),
                                  ALU.is_equal).then_inc(top_step, tops.one())
                dve.wait_ge(top_step, rested)
                dve.tensor_copy(part[:, 1, :], rest[:, :]).then_inc(top_step, tops.one())
                dve.wait_ge(top_step, tops.now())
                dve.tensor_tensor(rest[:, :], rest[:, :], part[:, 1, :], ALU.subtract).then_inc(top_step, tops.one())
                rested = tops.now()
                dve.tensor_tensor(Y[:, s], iota_k, keys_b[:, 1, :].unsqueeze(1).to_broadcast([P, NK, HK]),
                                  ALU.is_equal).then_inc(top_step, tops.one())
                dve.wait_ge(top_step, rested)
                dve.tensor_copy(part[:, 2, :], rest[:, :]).then_inc(top_step, tops.one())
                dve.wait_ge(top_step, tops.now())
                dve.tensor_tensor(WG[:, :, :, :], part[:, :, :].unsqueeze(2).to_broadcast([P, PARTS, GROUPS, HK]),
                                  group[:, :, :].unsqueeze(1).to_broadcast([P, PARTS, GROUPS, HK]), ALU.mult)\
                    .then_inc(top_step, tops.one())
                dve.wait_ge(top_step, tops.now())
                for q in range(PARTS):
                    last = dve.tensor_tensor(XW[:, s, q], onehot1.unsqueeze(1).to_broadcast([P, GROUPS, ROWS, HK]),
                                             WG[:, q].unsqueeze(2).to_broadcast([P, GROUPS, ROWS, HK]), ALU.mult)
                last.then_inc(xw_ready, 1)
                tops.end()

            def weigh(b, s):
                dve.wait_ge(g_ready, b * (ROWS // 2) + ROWS // 2)
                dve.wait_ge(w_ps, b * TB + s + 1)
                mine = GT[:, :, s * P:s * P + P].rearrange("p r (g j) -> p r g j", g=GROUPS)
                dve.tensor_tensor(mine, mine, W_ps.rearrange("p j g r -> p r g j"), ALU.mult)\
                   .then_inc(gw_ready, 1)

            def finish(b, s):
                dve.wait_ge(up_ps, b * TB + s + 1)
                dve.wait_ge(stored, b * (16 * TB) + 1)
                apart()
                dve.scalar_tensor_tensor(fin[:, s, :], out_ps[s], gains[:, 3:4], tile(b * TB + s), ALU.mult, ALU.add)\
                   .then_inc(fin_ready, 1)

            def experts(b, more):
                if more:
                    dve.wait_ge(xnT_ps, b + 1)
                    normed(xl, (b + 1) * TB, 2 * B + 3, xn_ready)
                top_keys(b, 1)
                weigh(b, 0)
                if more:
                    weigh(b, 1)
                    top_keys(b + 1, 0)
                else:
                    finish(b, 0)
                    weigh(b, 1)
                if more:
                    finish(b, 0)
                finish(b, 1)

            dve.wait_ge(iota_ready, 1 + GROUPS)
            dve.wait_ge(iota_k_ready, 1)
            top_keys(0, 0)
            with dve.Fori(0, B - 1) as b:
                experts(b, True)
            experts(B - 1, False)

        @block.tensor
        def _(pe):
            def turn(dst, src, signal):
                for i in range(2):
                    for j in range(2):
                        last = pe.transpose(dst[:, j, i * P:i * P + P], src[:, i, j * P:j * P + P], ident[:, :])
                last.then_inc(signal, 1)

            pe.wait_ge(ld_front, 32)
            for n in range(2 * NC):
                c, h = n // 2, n % 2
                if n == 1:
                    pe.wait_ge(ld_front2, 16)
                pe.matmul(front_ps[:, c, h * 512:h * 512 + 512], in_w[:, c * P:c * P + P], ctxT[:, h * 512:h * 512 + 512],
                          start=True, stop=True).then_inc(in_ps, 1)
            pe.wait_ge(ld_small2, 16 * 9)
            pe.wait_ge(u_ready, NC)
            for h in range(T // 512):
                for c in range(NC):
                    last = pe.matmul(ps[0:XD, 4 + h, :], xp_w[:, c, :], u[:, c, h * 512:h * 512 + 512],
                                     start=(c == 0), stop=(c == NC - 1))
                last.then_inc(xd_ps, 1)
            for n in range(2 * NC):
                c, h = n // 2, n % 2
                pe.wait_ge(xd_ready, 2)
                pe.wait_ge(xpad_ready, 2 * NC)
                pe.matmul(front_ps[:, c, h * 512:h * 512 + 512], dt_w[:, c * P:c * P + P], xdbl[0:DR, h * 512:h * 512 + 512],
                          start=True, stop=True).then_inc(dt_ps, 1)

            def project(i):
                pe.matmul(mm_ps[:, 0, :], wqT[:, :], ctxT[:, ds(i * S, S)], start=True, stop=True)
                pe.matmul(mm_ps[:, 1, :], wkT[:, :], ctxT[:, ds(i * S, S)], start=True, stop=True).then_inc(qk_ps, 1)

            def turn_xl(i):
                pe.wait_ge(xl_ready, i * TB + TB)
                turn(T_ps, xl, xlT_ps)

            def energy(i):
                pe.wait_ge(qk_ready, i * 2 + 2)
                for m in range(TB):
                    last = pe.matmul(mm_ps[:, m, :], qT[:, m * P:m * P + P], kT[:, :], start=True, stop=True)
                last.then_inc(e_ps, 1)

            def turn_att(i):
                pe.wait_ge(att_ready, i * TB + TB)
                pe.wait_ge(xlT_ready, i + 1)
                turn(T_ps, att, attT_ps)

            def mix(i):
                pe.wait_ge(attT_ready, i + 1)
                for l in range(TB):
                    for k in range(TB):
                        last = pe.matmul(mm_ps[:, l, :], xlT[:, k, l * P:l * P + P], attT[:, k, :],
                                         start=(k == 0), stop=(k == TB - 1))
                last.then_inc(xm_ps, 1)

            def turn_x2(i):
                pe.wait_ge(xl2_ready, i * TB + TB)
                turn(T_ps, xl, xl2T_ps)

            pe.wait_ge(consts_ready, 1)
            pe.wait_ge(ld_attn, 64)
            turn_xl(0)
            project(0)
            energy(0)
            pe.wait_ge(spv_ready, NC)
            pe.wait_ge(d_ready, NC)
            for c in range(NC):
                for h in range(2):
                    pe.matmul(y_ps[:, c, h * 512:h * 512 + 512], ident_d[:, c, :], u[:, c, h * 512:h * 512 + 512],
                              start=True, stop=False, skip_group_check=True)
            turn_att(0)
            mix(0)
            turn_x2(0)
            pe.wait_ge(ld_ffn, 64)
            pe.sem_inc(y_added, 2)

            def merged(b, more):
                def add_y(j):
                    pe.wait_ge(paired, b * (UNITS // 2) + j + 1)
                    c = j % 2
                    for h in range(2):
                        last = pe.matmul(y_ps[:, c, h * 512:h * 512 + 512], ident[:, :], hc[:, c, h * 512:h * 512 + 512],
                                         start=False, stop=False, skip_group_check=True)
                    last.then_inc(y_added, 1)

                def gate_up(i):
                    m, s = chunk(i), i % 2
                    if i >= 2:
                        pe.wait_ge(hdn_ready, b * NI + i - 1)
                    for n, w in enumerate((gate_w, up_w)):
                        for k in range(DK_F):
                            last = pe.matmul(ps[0:m, 6 + s, n * S:n * S + S], w[:, k, i * P:i * P + m], x2T[:, k, :],
                                             start=(k == 0), stop=(k == DK_F - 1))
                    last.then_inc(gu_ps, 1)

                def down(b):
                    pe.wait_ge(hdn_ready, b * NI + NI)
                    for t in range(TB):
                        for i in range(NI):
                            m = chunk(i)
                            last = pe.matmul(down_ps_v[:, t, :], hdn[0:m, i, t * P:t * P + P], down_w[0:m, i, :],
                                             start=(i == 0), stop=(i == NI - 1))
                    last.then_inc(down_ps, 1)

                pe.wait_ge(xl2T_ready, b + 1)
                gate_up(0)
                if more:
                    project(b + 1)
                gate_up(1)
                if more:
                    turn_xl(b + 1)
                gate_up(2)
                if more:
                    energy(b + 1)
                gate_up(3)
                gate_up(4)
                add_y(0)
                add_y(1)
                gate_up(5)
                if more:
                    turn_att(b + 1)
                    mix(b + 1)
                down(b)
                add_y(2)
                if more:
                    turn_x2(b + 1)
                add_y(3)

            with pe.Fori(0, B - 1) as b:
                merged(b, True)
            merged(B - 1, False)

            def gate_out(i):
                pe.wait_ge(yz_ready, i + 1 if i < 2 else B)
                turn(ps[:, GATE_BANKS[i], :].rearrange("p (k s) -> p k s", k=2), gated[:, :, i * S:i * S + S], yzT_ps)

            def scores(i, s):
                pe.wait_ge(q_ready, i * 2 + 2)
                for side in range(2):
                    if s:
                        pe.wait_ge(sim_ready, i * 2 * TB + side + 1)
                    half = slice(side * DK, side * DK + DK)
                    for h in range(H):
                        last = pe.matmul(ps[:, 5 + side, h * NK:h * NK + NK], qTp[half, h, s * P:s * P + P],
                                         keysT[half, h, :], start=True, stop=True)
                    last.then_inc(sim_ps, 1)

            def turn_xn(i):
                pe.wait_ge(xn_ready, i * TB + TB)
                turn(T_ps, xl, xnT_ps)

            def queries(i):
                pe.wait_ge(xnT_ready, i + 1)
                for n in range(2):
                    for h in range(2 * n, 2 * n + 2):
                        for k in range(DK_F):
                            last = pe.matmul(ps[:, 5 + n, (h % 2) * S:(h % 2) * S + S], wqp[:, k, h * P:h * P + P], xnT[:, k, :],
                                             start=(k == 0), stop=(k == DK_F - 1))
                    last.then_inc(q_ps, 1)

            def down(b, n):
                if n < 2:
                    pe.wait_ge(sim_ready, b * 2 * TB + 2 * TB - 1 + n)
                else:
                    pe.wait_ge(g_ready, b * (ROWS // 2) + n - 1)
                for r in range(2):
                    row = 2 * n + r
                    for k in range(DK_F):
                        last = pe.matmul(ps[:, 5 + n % 2, r * S:r * S + S], e_down[:, k, row * NK:row * NK + NK], xnT[:, k, :],
                                         start=(k == 0), stop=(k == DK_F - 1))
                last.then_inc(g_ps, 1)

            def weights(b, s):
                pe.wait_ge(xw_ready, b * TB + s + 1)
                if s:
                    pe.wait_ge(gw_ready, b * TB + s)
                for j in range(HK):
                    for q in range(PARTS):
                        last = pe.matmul(W_ps[:, j].rearrange("p g r -> p (g r)"), Y[:, s, :, j],
                                         XW[:, s, q, :, :, j].rearrange("p g r -> p (g r)"),
                                         start=(q == 0), stop=(q == PARTS - 1))
                last.then_inc(w_ps, 1)

            def up(b, s):
                pe.wait_ge(gw_ready, b * TB + s + 1)
                for r in range(ROWS):
                    last = pe.matmul(out_ps[s], GT[:, r, s * P:s * P + P], e_up[:, r, :], start=(r == 0), stop=(r == ROWS - 1))
                last.then_inc(up_ps, 1)

            def experts(b, more):
                for n in range(ROWS // 2):
                    down(b, n)
                if more:
                    turn_xn(b + 1)
                weights(b, 0)
                pe.wait_ge(g_ready, b * (ROWS // 2) + ROWS // 2)
                if more:
                    queries(b + 1)
                    weights(b, 1)
                    scores(b + 1, 0)
                    up(b, 0)
                    scores(b + 1, 1)
                    up(b, 1)
                else:
                    up(b, 0)
                    weights(b, 1)
                    up(b, 1)

            pe.wait_ge(ld_keys, 32)
            pe.wait_ge(ld_exp, 32)
            for i in range(B):
                gate_out(i)
            turn_xn(0)
            queries(0)
            scores(0, 0)
            scores(0, 1)
            with pe.Fori(0, B - 1) as b:
                experts(b, True)
            experts(B - 1, False)


def columns(v, n):
    full = np.zeros((n * P,), v.dtype)
    full[:v.size] = v.reshape(-1)
    return np.ascontiguousarray(full.reshape(n, P).T)


def kernel(**inputs):
    import concourse.bacc as bacc
    from concourse.bass_utils import run_bass_kernel_spmd

    a = {k: np.asarray(v) for k, v in inputs.items()}
    t = lambda m: np.ascontiguousarray(m.T)
    arrays = {
        "x": np.ascontiguousarray(a["x"].reshape(T, D)),
        "ctxT": t(a["ctx_1024"].reshape(T, CTX)),
        "gates": np.concatenate([a["g_xattn"], a["g_ffn"]]).reshape(1, 4),
        "wqT": t(a["L0_xattn_Wq"]), "wkT": t(a["L0_xattn_Wk"]),
        "bq": a["L0_xattn_bq"].reshape(P, 1), "bk": a["L0_xattn_bk"].reshape(P, 1),
        "gate_wT": t(a["L0_ffn_gate_w"]), "up_wT": t(a["L0_ffn_up_w"]), "down_wT": t(a["L0_ffn_down_w"]),
        "gate_s": columns(a["L0_ffn_gate_s"], NI), "up_s": columns(a["L0_ffn_up_s"], NI),
        "down_s": a["L0_ffn_down_s"].reshape(1, D),
        "in_wT": t(a["L1_xattn_in_proj_w"]), "conv_w": a["L1_xattn_conv_w"],
        "conv_b": columns(a["L1_xattn_conv_b"], NC),
        "xp_wT": t(a["L1_xattn_x_proj_w"]), "dt_wT": t(a["L1_xattn_dt_proj_w"]),
        "dt_b": columns(a["L1_xattn_dt_proj_b"], NC), "A_log": a["L1_xattn_A_log"],
        "D": columns(a["L1_xattn_D"], NC),
        "wqp": a["L1_ffn_Wq"],
        "keysT": np.ascontiguousarray(a["L1_ffn_keys"].transpose(2, 3, 0, 1).reshape(2 * DK, H * NK)),
        "e_downT": t(a["L1_ffn_e_down"]), "e_up": a["L1_ffn_e_up"],
    }
    arrays = {k: np.ascontiguousarray(v) for k, v in arrays.items()}
    nc = bacc.Bacc("TRN2", target_bir_lowering=False, num_devices=1)
    io = {k: nc.dram_tensor(k, v.shape, mybir.dt.float32, kind="ExternalInput").ap() for k, v in arrays.items()}
    out = nc.dram_tensor("out", (T, D), mybir.dt.float32, kind="ExternalOutput").ap()
    build(nc, io, out)
    got = run_bass_kernel_spmd(nc, [arrays], core_ids=[0]).results[0]["out"]
    return np.asarray(got).reshape(B, S, D)
```

```python
import numpy as np
import concourse.bass as bass
from concourse import mybir
from contextlib import ExitStack

P = 128
B, S, D = 4, 256, 256
CTX = 128
T = B * S
NT = T // P
TB = S // P
DK_F = D // P
INTER = 704
NI = (INTER + P - 1) // P
LAST = INTER - (NI - 1) * P
DI, DS, DC, DR = 256, 16, 4, 8
NC = DI // P
XD = DR + 2 * DS
H, K, DK, NK, E = 4, 8, 64, 128, 2048
ROWS = E // NK
HK = H * K
EPS = 1e-5
NPB = DS // B
UNITS = NPB * NC
SLOTS = 4
PAD = S + DC - 1
GATE_BANKS = (4, 7, 0, 1)
GROUPS = P // HK
PARTS = 3


def build(nc, io, out):
    f32, b16, u32, i32 = mybir.dt.float32, mybir.dt.bfloat16, mybir.dt.uint32, mybir.dt.int32
    ALU, ACT, AX = mybir.AluOpType, mybir.ActivationFunctionType, mybir.AxisListType
    ds = bass.ds
    ctx = ExitStack()
    with ctx:
        def sb(name, shape, dt=f32):
            return ctx.enter_context(nc.sbuf_tensor("sb_" + name, shape, dt))

        def sem(name):
            return ctx.enter_context(nc.semaphore(name))

        x = sb("x", [P, NT * D])
        ctxT = sb("ctxT", [P, T])
        wqT, wkT = sb("wqT", [P, P]), sb("wkT", [P, P])
        bq, bk = sb("bq", [P, 1]), sb("bk", [P, 1])
        gate_w, up_w = sb("gate_w", [P, DK_F, INTER]), sb("up_w", [P, DK_F, INTER])
        down_w = sb("down_w", [P, NI, D])
        gate_s, up_s, half_gs = sb("gate_s", [P, NI]), sb("up_s", [P, NI]), sb("half_gs", [P, NI])
        down_s, dsg = sb("down_s", [P, D]), sb("dsg", [P, D])
        in_w = sb("in_w", [P, DI])
        conv_w, conv_b = sb("conv_w", [P, NC, DC]), sb("conv_b", [P, NC])
        xp_w = sb("xp_w", [P, NC, XD])
        dt_w, dt_b = sb("dt_w", [DR, DI]), sb("dt_b", [P, NC])
        A = sb("A", [P, NC * DS])
        Dp = sb("Dp", [P, NC])
        wqp = sb("wqp", [P, DK_F, H * P])
        keysT = sb("keysT", [P, H, NK])
        e_down = sb("e_down", [P, DK_F, E])
        e_up = sb("e_up", [P, ROWS, D])
        gains = sb("gains", [P, 4])
        ident = sb("ident", [P, P])
        ident_d = sb("ident_d", [P, NC, P])
        iota_i = sb("iota_i", [P, P], i32)
        iota_f = sb("iota_f", [P, P])
        group = sb("group", [P, GROUPS, HK], b16)
        minus_half = sb("minus_half", [P, NT])
        zero = sb("zero", [P, B])
        stats = sb("stats", [P, NT, 6])
        mv = sb("mv", [P, NT, 2])
        mean = sb("mean", [P, NT])
        veps, rstd = sb("veps", [P, NT]), sb("rstd", [P, NT])
        xl = sb("xl", [P, TB, D])
        xlT = sb("xlT", [P, DK_F, S])
        qT, kT = sb("qT", [P, S]), sb("kT", [P, S])
        neg_max, row_sum, row_inv = sb("neg_max", [P, TB]), sb("row_sum", [P, TB]), sb("row_inv", [P, TB])
        att = sb("att", [P, TB, S])
        attT = sb("attT", [P, TB, S])
        th = sb("th", [P, 2, S])
        ga = sb("ga", [P, 2, S])
        x2T = sb("x2T", [P, DK_F, S])
        hdn = sb("hdn", [P, NI, S])
        u = sb("u", [P, NC, T])
        delta = sb("delta", [P, NC, T])
        du = sb("du", [P, NC, T])
        xdbl = sb("xdbl", [XD, T])
        arena = sb("arena", [P, 18 * T])
        xpad = arena[:, 0:NC * B * PAD].rearrange("p (c b s) -> p c b s", c=NC, b=B)
        conv = arena[:, 3 * T:5 * T].rearrange("p (c b s) -> p c b s", c=NC, b=B)
        sp_v = arena[:, 12 * T:14 * T].rearrange("p (c t) -> p c t", c=NC)
        sp_e = arena[:, 8 * T:10 * T].rearrange("p (c t) -> p c t", c=NC)
        sp_w = arena[:, 10 * T:12 * T].rearrange("p (c t) -> p c t", c=NC)
        sp_l = arena[:, 2 * T:4 * T].rearrange("p (c t) -> p c t", c=NC)
        sp_i = arena[:, 6 * T:8 * T].rearrange("p (c t) -> p c t", c=NC)
        dA = arena[:, 0:4 * T].rearrange("p (s t) -> p s t", s=SLOTS)
        dBu = arena[:, 4 * T:8 * T].rearrange("p (s t) -> p s t", s=SLOTS)
        hs = arena[:, 8 * T:10 * T].rearrange("p (s t) -> p s t", s=2)
        hc = arena[:, 10 * T:14 * T].rearrange("p (s t) -> p s t", s=SLOTS)
        bbc = arena[:, 14 * T:16 * T].rearrange("p (s t) -> p s t", s=2)
        cbc = arena[:, 16 * T:18 * T].rearrange("p (s t) -> p s t", s=2)
        GT = arena[:, 0:4 * T].rearrange("p (r t) -> p r t", r=ROWS)
        Y = arena[:, 4 * T:8 * T].bitcast(b16).rearrange("p (s k j) -> p s k j", s=TB, k=NK)
        XW = arena[:, 8 * T:14 * T].bitcast(b16).rearrange("p (s q g r j) -> p s q g r j", s=TB, q=PARTS, g=GROUPS, r=ROWS)
        iota_k = arena[:, 16 * T:18 * T].bitcast(b16).rearrange("p (k j) -> p k j", k=NK)
        sims = du[:, :, :].rearrange("p c t -> p (c t)").rearrange("p (s n k) -> p s n k", s=TB, k=NK)
        xnT = arena[:, 14 * T:14 * T + DK_F * S].rearrange("p (k t) -> p k t", k=DK_F)
        qTp = arena[:, 15 * T:16 * T].rearrange("p (h t) -> p h t", h=H)
        gated = u
        spare = delta[:, :, :].rearrange("p c t -> p (c t)")
        fin = spare[:, 0:TB * D].rearrange("p (s d) -> p s d", s=TB)
        onehot1 = spare[:, T:T + HK * ROWS // 2].bitcast(b16).rearrange("p (r j) -> p r j", r=ROWS)
        NS = 2 * H
        top = sb("top", [P, NS, K])
        topi = sb("topi", [P, NS, K], u32)
        topf = sb("topf", [P, NS, K])
        cand = sb("cand", [P, H, K, K])
        best = sb("best", [P, H, K])
        pk = sb("pk", [P, H, K], u32)
        pab = sb("pab", [P, 2, HK], u32)
        pabf = sb("pabf", [P, 2 * HK])
        eq = sb("eq", [P, NS, K, K])
        picked = sb("picked", [P, 2 * HK])
        over = sb("over", [P, HK])
        V = sb("V", [P, 3, HK])
        VT = sb("VT", [P, 3, HK])
        rest = sb("rest", [P, HK])
        keys_b = sb("keys_b", [P, 2, HK], b16)
        part = sb("part", [P, PARTS, HK], b16)
        WG = sb("WG", [P, PARTS, GROUPS, HK], b16)

        ps = ctx.enter_context(nc.psum_tensor("ps", [P, 8, 512], f32))
        y_ps = ps[:, 0:4, :].rearrange("p (c h) s -> p c (h s)", c=NC)
        front_ps = y_ps
        T_ps = ps[:, 4, :].rearrange("p (k s) -> p k s", k=2)
        mm_ps = ps[:, 5, :].rearrange("p (k s) -> p k s", k=2)
        down_ps_v = ps[:, 6, :].rearrange("p (k s) -> p k s", k=2)
        out_ps = [ps[:, 7, 0:D], ps[:, 4, 0:D]]
        W_ps = ps[:, 0:4, :].rearrange("p b (j g r) -> p (b j) g r", g=GROUPS, r=ROWS)

        scratch = nc.dram_tensor("bc_scratch", [2 * DS, T], f32, kind="Internal").ap()

        ld_x, ld_front, ld_small, ld_attn, ld_ffn = (sem("ld_" + n) for n in ("x", "front", "small", "attn", "ffn"))
        ld_keys, ld_exp = sem("ld_keys"), sem("ld_exp")
        consts_ready, iota_ready, pads_ready = sem("consts_ready"), sem("iota_ready"), sem("pads_ready")
        act_step, pool_step = sem("act_step"), sem("pool_step")
        front_step, attn_step, feed_step, keys_step = (sem(n + "_step") for n in ("front", "attn", "feed", "keys"))
        decayed, paired, ld_front2, ld_small2, ld_xp = sem("decayed"), sem("paired"), sem("ld_front2"), sem("ld_small2"), sem("ld_xp")
        ga_scaled, d_ready, top_step = sem("ga_scaled"), sem("d_ready"), sem("top_step")
        iota_k_ready, dsg_ready, down_w_ready = sem("iota_k_ready"), sem("dsg_ready"), sem("down_w_ready")
        dve_passed, pool_passed = sem("dve_passed"), sem("pool_passed")
        veps_ready, rstd_ready = sem("veps_ready"), sem("rstd_ready")
        gains_ready = sem("gains_ready")
        in_ps, xpad_ready, conv_ready, u_ready = sem("in_ps"), sem("xpad_ready"), sem("conv_ready"), sem("u_ready")
        xd_ps, xd_ready, xd_stored, dt_ps = sem("xd_ps"), sem("xd_ready"), sem("xd_stored"), sem("dt_ps")
        spv_ready, spe_ready, spw_ready = sem("spv_ready"), sem("spe_ready"), sem("spw_ready")
        spa_ready, spl_ready, spi_ready, a_ready = sem("spa_ready"), sem("spl_ready"), sem("spi_ready"), sem("a_ready")
        delta_ready, du_ready = sem("delta_ready"), sem("du_ready")
        b_loaded = [sem("b_loaded0"), sem("b_loaded1")]
        c_loaded = [sem("c_loaded0"), sem("c_loaded1")]
        da_ready, dbu_ready, scanned, hc_ready, y_added = (sem(n) for n in (
            "da_ready", "dbu_ready", "scanned", "hc_ready", "y_added"))
        xl_ready, xlT_ps, xlT_ready = sem("xl_ready"), sem("xlT_ps"), sem("xlT_ready")
        qk_ps, qk_ready, e_ps, max_ready, exp_ready = (sem(n) for n in (
            "qk_ps", "qk_ready", "e_ps", "max_ready", "exp_ready"))
        att_ready, attT_ps, attT_ready, xm_ps = (sem(n) for n in ("att_ready", "attT_ps", "attT_ready", "xm_ps"))
        xl2_ready, xl2T_ps, xl2T_ready = sem("xl2_ready"), sem("xl2T_ps"), sem("xl2T_ready")
        gu_ps, gate_act, hdn_ready, down_ps, x2_ready = (sem(n) for n in (
            "gu_ps", "gate_act", "hdn_ready", "down_ps", "x2_ready"))
        zl_ready, sz_ready, yz_ready, yzT_ps = (sem(n) for n in ("zl_ready", "sz_ready", "yz_ready", "yzT_ps"))
        xn_ready, xnT_ps, xnT_ready = sem("xn_ready"), sem("xnT_ps"), sem("xnT_ready")
        q_ps, q_ready, sim_ps, sim_ready, g_ps, g_ready = (sem(n) for n in (
            "q_ps", "q_ready", "sim_ps", "sim_ready", "g_ps", "g_ready"))
        xw_ready, w_ps, gw_ready, up_ps, fin_ready, stored = (sem(n) for n in (
            "xw_ready", "w_ps", "gw_ready", "up_ps", "fin_ready", "stored"))

        block = ctx.enter_context(nc.Block())

        class Steps:

            def __init__(self, per=0):
                self.per, self.base, self.inner = per, 0, 0

            def begin(self, i):
                self.base, self.inner = i * self.per, 0

            def one(self):
                self.inner += 1
                return 1

            def now(self):
                return self.base + self.inner

            def end(self):
                assert self.inner == self.per, (self.inner, self.per)

        def chunk(i):
            return P if i < NI - 1 else LAST


        @block.sync
        def _(sp):
            sp.dma_start(ctxT[:, 0:T // 2], io["ctxT"][:, 0:T // 2]).then_inc(ld_front, 16)
            sp.dma_start(in_w[:, :], io["in_wT"]).then_inc(ld_front, 16)
            sp.dma_start(ctxT[:, T // 2:T], io["ctxT"][:, T // 2:T]).then_inc(ld_front2, 16)
            sp.dma_start(x[:, :].rearrange("p (t d) -> p t d", d=D),
                         io["x"].rearrange("(t p) d -> p t d", p=P)).then_inc(ld_x, 16)
            sp.dma_start(wqT[:, :], io["wqT"]).then_inc(ld_attn, 16)
            sp.dma_start(wkT[:, :], io["wkT"]).then_inc(ld_attn, 16)
            sp.dma_start(bq[:, :], io["bq"]).then_inc(ld_attn, 16)
            sp.dma_start(bk[:, :], io["bk"]).then_inc(ld_attn, 16)
            sp.dma_start(gate_w[:, :, :], io["gate_wT"].rearrange("(k p) n -> p k n", p=P)).then_inc(ld_ffn, 16)
            sp.dma_start(up_w[:, :, :], io["up_wT"].rearrange("(k p) n -> p k n", p=P)).then_inc(ld_ffn, 16)
            full = (NI - 1) * P
            sp.dma_start(down_w[:, 0:NI - 1, :], io["down_wT"][0:full, :].rearrange("(k p) n -> p k n", p=P)).then_inc(ld_ffn, 16)
            sp.dma_start(down_w[0:LAST, NI - 1, :], io["down_wT"][full:INTER, :]).then_inc(ld_ffn, 16)
            sp.wait_ge(xd_ready, T // 512)
            sp.dma_start(scratch, xdbl[DR:XD, :]).then_inc(xd_stored, 16)
            sp.wait_ge(xd_stored, 16)

            def spread_b(row, slot):
                sp.dma_start(bbc[:, slot, :], scratch[row, :].broadcast_to([P, T])).then_inc(b_loaded[slot], 16)

            def spread_c(row, slot):
                sp.dma_start(cbc[:, slot, :], scratch[row, :].broadcast_to([P, T])).then_inc(c_loaded[slot], 16)

            for state in range(2):
                spread_b(slice(state, state + 1), state)
                spread_c(slice(DS + state, DS + state + 1), state)

            def next_b(state, row, slot):
                sp.wait_ge(dbu_ready, state * NC - NC)
                spread_b(row, slot)

            def next_c(state, row, slot):
                sp.wait_ge(hc_ready, state * NC - NC)
                spread_c(row, slot)

            next_b(2, slice(2, 3), 0)
            with sp.Fori(0, (DS - 3) // 2) as m:
                for n in range(2):
                    next_b(m * 2 + (3 + n), ds(m * 2 + (3 + n), 1), (3 + n) % 2)
                    next_c(m * 2 + (2 + n), ds(m * 2 + (2 + n + DS), 1), n)
            next_b(DS - 1, slice(DS - 1, DS), 1)
            for state in range(DS - 2, DS):
                next_c(state, slice(DS + state, DS + state + 1), state % 2)
            sp.sem_inc(stored, 1)
            with sp.Fori(0, B) as b:
                for s in range(TB):
                    sp.wait_ge(fin_ready, b * TB + s + 1)
                    sp.dma_start(out.rearrange("(t p) d -> p t d", p=P)[:, ds(b * TB + s, 1), :],
                                 fin[:, s:s + 1, :]).then_inc(stored, 16)
            sp.wait_ge(stored, 16 * NT + 1)

        @block.gpsimd
        def _(pool):
            pool.memset(xpad[:, :, :, 0:DC - 1], 0.0).then_inc(pads_ready, 1)
            pool.memset(zero[:, :], 0.0).then_inc(pads_ready, 1)
            pool.memset(minus_half[:, :], -0.5).then_inc(pool_step, 1)
            pool.memset(ident[:, :], 0.0).then_inc(pool_step, 1)
            pool.wait_ge(pool_step, 2)
            pool.affine_select(out=ident[:, :], in_=ident[:, :], compare_op=ALU.not_equal, fill=1.0,
                               base=0, pattern=[[-1, P]], channel_multiplier=1).then_inc(consts_ready, 1)
            pool.iota(iota_i[:, :], pattern=[[1, P]], base=0, channel_multiplier=0).then_inc(pool_step, 1)
            pool.wait_ge(pool_step, 3)
            pool.tensor_copy(iota_f[:, :], iota_i[:, :]).then_inc(iota_ready, 1)
            pool.memset(group[:, :, :], 0.0).then_inc(pool_step, 1)
            pool.wait_ge(pool_step, 4)
            for g in range(GROUPS):
                pool.memset(group[g * HK:g * HK + HK, g, :], 1.0).then_inc(iota_ready, 1)
            pool.wait_ge(iota_ready, 1 + GROUPS)

            def power(first, tiles, n):
                pool.wait_ge(veps_ready, n)
                pool.sem_inc(pool_passed, 1)
                pool.tensor_tensor(rstd[:, ds(first, tiles)], veps[:, ds(first, tiles)], minus_half[:, 0:tiles], ALU.pow)\
                    .then_inc(rstd_ready, 1)

            def times_b(b, k):
                state, c = k // NC, k % NC
                pool.wait_ge(b_loaded[state % 2], b * (NPB // 2 * 16) + 16 * (state // 2 + 1))
                pool.wait_ge(scanned, b * UNITS + k + 1)
                pool.tensor_tensor(dBu[:, k % SLOTS, :], du[:, c, :], bbc[:, state % 2, :], ALU.mult)\
                    .then_inc(dbu_ready, 1)

            def add_pair(b, j):
                k = (j // 2) * SLOTS + j % 2
                pool.wait_ge(hc_ready, b * UNITS + k + NC + 1)
                pool.tensor_tensor(hc[:, k % SLOTS, :], hc[:, k % SLOTS, :], hc[:, (k + NC) % SLOTS, :], ALU.add)\
                    .then_inc(paired, 1)

            for dst, name in ((dt_b, "dt_b"), (Dp, "D"), (gate_s, "gate_s"), (up_s, "up_s")):
                pool.dma_start(dst[:, :], io[name]).then_inc(ld_small2, 16)
            pool.dma_start(A[:, :].rearrange("p (c n) -> p c n", c=NC),
                           io["A_log"].rearrange("(c p) n -> p c n", p=P)).then_inc(ld_small2, 16)
            pool.dma_start(gains[:, :], io["gates"].broadcast_to([P, 4])).then_inc(ld_small2, 16)
            pool.dma_start(down_s[:, :], io["down_s"].broadcast_to([P, D])).then_inc(ld_small2, 16)
            power(0, NT, 1)
            pool.wait_ge(ld_ffn, 64)
            pool.wait_ge(dsg_ready, 1)
            for rows, part_w in ((slice(0, P), slice(0, NI - 1)), (slice(0, LAST), slice(NI - 1, NI))):
                scaled = down_w[rows, part_w, :]
                pool.tensor_tensor(scaled, scaled, dsg[rows, :].unsqueeze(1).to_broadcast(list(scaled.shape)), ALU.mult)\
                    .then_inc(down_w_ready, 1)
            pool.wait_ge(rstd_ready, 1)
            power(0, TB, 2)

            def merged(b, more):
                times_b(b, 0)
                times_b(b, 1)
                times_b(b, 2)
                times_b(b, 3)
                times_b(b, 4)
                times_b(b, 5)
                add_pair(b, 0)
                add_pair(b, 1)
                times_b(b, 6)
                times_b(b, 7)
                add_pair(b, 2)
                if more:
                    power((b + 1) * TB, TB, b * 2 + 3)
                add_pair(b, 3)
                power(b * TB, TB, b * 2 + (4 if more else 3))

            with pool.Fori(0, B - 1) as b:
                merged(b, True)
            merged(B - 1, False)

            power(0, TB, 2 * B + 2)
            power(TB, NT - TB, 2 * B + 3)

        @block.scalar
        def _(act):
            act.dma_start(conv_w[:, :, :], io["conv_w"].rearrange("(c p) n -> p c n", p=P)).then_inc(ld_small, 16)
            act.dma_start(conv_b[:, :], io["conv_b"]).then_inc(ld_small, 16)
            act.dma_start(xp_w[:, :, :], io["xp_wT"].rearrange("(c p) n -> p c n", p=P)).then_inc(ld_xp, 16)
            act.dma_start(dt_w[:, :], io["dt_wT"]).then_inc(ld_xp, 16)

            act.wait_ge(pads_ready, 2)
            for h in range(2):
                act.wait_ge(in_ps, 2 * h + 2)
                act.copy(xpad[:, 1, 2 * h:2 * h + 2, DC - 1:PAD],
                         front_ps[:, 1, h * 512:h * 512 + 512].rearrange("p (b s) -> p b s", b=2)).then_inc(xpad_ready, 1)

            def copy_xlT(i):
                act.wait_ge(xlT_ps, i + 1)
                act.copy(xlT[:, :, :], T_ps).then_inc(xlT_ready, 1)

            def copy_qk(i):
                act.wait_ge(qk_ps, i + 1)
                act.activation(qT[:, :], mm_ps[:, 0, :], ACT.Identity, bias=bq[:, :]).then_inc(qk_ready, 1)
                act.activation(kT[:, :], mm_ps[:, 1, :], ACT.Identity, bias=bk[:, :]).then_inc(qk_ready, 1)

            def softmax_exp(i):
                act.wait_ge(max_ready, i + 1)
                for m in range(TB):
                    act.activation(att[:, m, :], mm_ps[:, m, :], ACT.Exp, bias=neg_max[:, m:m + 1],
                                   accum_out=row_sum[:, m:m + 1]).then_inc(exp_ready, 1)

            def copy_attT(i):
                act.wait_ge(attT_ps, i + 1)
                act.copy(attT[:, :, :], T_ps).then_inc(attT_ready, 1)

            def copy_x2T(i):
                act.wait_ge(xl2T_ps, i + 1)
                act.copy(x2T[:, :, :], T_ps).then_inc(xl2T_ready, 1)

            act.wait_ge(ld_attn, 64)
            copy_qk(0)
            act.wait_ge(ld_small, 32)

            def conv_silu(h):
                for c in range(NC):
                    act.wait_ge(conv_ready, h * NC + c + 1)
                    act.activation(u[:, c, h * 512:h * 512 + 512].rearrange("p (b s) -> p b s", b=2),
                                   conv[:, c, 2 * h:2 * h + 2, :], ACT.Silu, bias=conv_b[:, c:c + 1]).then_inc(u_ready, 1)

            def copy_xd(h):
                act.wait_ge(xd_ps, h + 1)
                act.copy(xdbl[:, h * 512:h * 512 + 512], ps[0:XD, 6 + h, :]).then_inc(xd_ready, 1)

            conv_silu(0)
            copy_xd(0)
            conv_silu(1)
            act.dma_start(wqp[:, :, :], io["wqp"].rearrange("(k p) n -> p k n", p=P)).then_inc(ld_keys, 16)
            act.dma_start(keysT[:, :, :], io["keysT"].rearrange("p (h k) -> p h k", h=H)).then_inc(ld_keys, 16)
            act.dma_start(e_down[:, :, :], io["e_downT"].rearrange("(k p) n -> p k n", p=P)).then_inc(ld_exp, 16)
            act.dma_start(e_up[:, :, :], io["e_up"].rearrange("(r p) n -> p r n", p=P)).then_inc(ld_exp, 16)
            act.wait_ge(ld_small2, 16 * 7)
            act.activation(gains[:, :], gains[:, :], ACT.Tanh).then_inc(gains_ready, 1)
            copy_xd(1)
            for c in range(NC):
                act.wait_ge(dt_ps, NC + c + 1)
                act.activation(sp_l[:, c, :], front_ps[:, c, :], ACT.Abs, bias=dt_b[:, c:c + 1]).then_inc(spa_ready, 1)
                act.wait_ge(spa_ready, c + 1)
                act.activation(sp_e[:, c, :], sp_l[:, c, :], ACT.Exp, scale=-1.0).then_inc(spe_ready, 1)
            for c in range(NC):
                act.activation(sp_i[:, c, :], sp_l[:, c, :], ACT.Tanh, scale=0.5).then_inc(spi_ready, 1)
                if c == 0:
                    softmax_exp(0)
                    copy_xlT(0)
            copy_attT(0)
            act.activation(sp_v[:, 0, :], front_ps[:, 0, :], ACT.Relu, bias=dt_b[:, 0:1]).then_inc(spv_ready, 1)
            for c in range(NC):
                act.wait_ge(spw_ready, c + 1)
                act.wait_ge(spi_ready, c + 1)
                act.activation(sp_l[:, c, :], sp_w[:, c, :], ACT.Ln).then_inc(spl_ready, 1)
                if c == 0:
                    act.activation(sp_v[:, 1, :], front_ps[:, 1, :], ACT.Relu, bias=dt_b[:, 1:2]).then_inc(spv_ready, 1)
            act.activation(A[:, :], A[:, :], ACT.Exp).then_inc(act_step, 1)
            act.wait_ge(act_step, 1)
            act.mul(A[:, :], A[:, :], -1.0).then_inc(a_ready, 1)
            copy_x2T(0)
            act.wait_ge(a_ready, 1)
            act.wait_ge(delta_ready, 1)

            def merged(b, more):
                def decay(k):
                    state, c = k // NC, k % NC
                    act.wait_ge(scanned, b * UNITS + k + 1)
                    act.activation(dA[:, k % SLOTS, :], delta[:, c, :], ACT.Exp,
                                   scale=A[:, ds(b * NPB + (c * DS + state), 1)]).then_inc(decayed, 1)
                    act.wait_ge(decayed, b * UNITS + k + 1)
                    act.copy(dA[:, k % SLOTS, 0:T:S], zero[:, :]).then_inc(da_ready, 1)

                def gate(i):
                    m, s = chunk(i), i % 2
                    act.wait_ge(gu_ps, b * NI + i + 1)
                    if i >= 2:
                        act.wait_ge(hdn_ready, b * NI + i - 1)
                    act.activation(th[0:m, s, :], ps[0:m, 6 + s, 0:S], ACT.Tanh, scale=half_gs[0:m, i:i + 1])\
                        .then_inc(gate_act, 1)
                    act.activation(ga[0:m, s, :], ps[0:m, 6 + s, 0:S], ACT.Copy, scale=half_gs[0:m, i:i + 1])\
                        .then_inc(gate_act, 1)

                decay(0)
                decay(1)
                gate(0)
                decay(2)
                gate(1)
                decay(3)
                decay(4)
                gate(2)
                if more:
                    copy_qk(b + 1)
                gate(3)
                decay(5)
                decay(6)
                gate(4)
                decay(7)
                if more:
                    softmax_exp(b + 1)
                    copy_xlT(b + 1)
                gate(5)
                if more:
                    copy_attT(b + 1)
                    copy_x2T(b + 1)

            with act.Fori(0, B - 1) as b:
                merged(b, True)
            merged(B - 1, False)

            for n, batches in enumerate((slice(0, (B - 1) * S), slice((B - 1) * S, B * S))):
                act.wait_ge(zl_ready, (B - 1 + n) * TB)
                act.activation(gated[:, :, batches], gated[:, :, batches], ACT.Silu).then_inc(sz_ready, 1)

            act.wait_ge(y_added, B * UNITS // 2 + 2)
            act.wait_ge(iota_ready, 1 + GROUPS)
            act.copy(iota_k, iota_f[:, :].unsqueeze(2).to_broadcast([P, NK, HK])).then_inc(iota_k_ready, 1)

            def keys_in(i):
                act.wait_ge(xnT_ps, i + 1)
                act.copy(xnT, T_ps).then_inc(xnT_ready, 1)
                for n in range(2):
                    act.wait_ge(q_ps, i * 2 + n + 1)
                    act.copy(qTp[:, 2 * n:2 * n + 2, :], ps[:, 5 + n, :].rearrange("p (h t) -> p h t", h=2)).then_inc(q_ready, 1)

            def copy_sims(i, s):
                for side in range(2):
                    act.wait_ge(sim_ps, i * 2 * TB + 2 * s + side + 1)
                    act.copy(sims[:, s, side * H:side * H + H, :],
                             ps[:, 5 + side, :].rearrange("p (h k) -> p h k", h=H)).then_inc(sim_ready, 1)

            def experts(b, more):
                for n in range(ROWS // 2):
                    act.wait_ge(g_ps, b * (ROWS // 2) + n + 1)
                    act.activation(GT[:, 2 * n:2 * n + 2, :], ps[:, 5 + n % 2, :].rearrange("p (r t) -> p r t", r=2),
                                   ACT.Silu).then_inc(g_ready, 1)
                if more:
                    keys_in(b + 1)
                    copy_sims(b + 1, 0)
                    act.wait_ge(xw_ready, b * TB + TB)
                    copy_sims(b + 1, 1)

            keys_in(0)
            copy_sims(0, 0)
            copy_sims(0, 1)
            with act.Fori(0, B - 1) as b:
                experts(b, True)
            experts(B - 1, False)

        @block.vector
        def _(dve):
            front = Steps()
            attn = Steps(3 + 2 * TB)
            feed = Steps(1 + 2 * TB)
            keys = Steps()
            tops = Steps(45)

            def apart():
                dve.sem_inc(dve_passed, 1)

            def tile(i, n=1):
                return x[:, ds(i * D, n * D)]

            def sums(st, st_step, first, n):
                apart()
                for t in range(n):
                    dve.bn_stats(stats[:, t, :], tile(first + t)).then_inc(st_step, st.one())
                dve.wait_ge(st_step, st.now())
                apart()
                for t in range(n):
                    dve.bn_aggr(mv[:, t, :], stats[:, t, :]).then_inc(st_step, st.one())
                dve.wait_ge(st_step, st.now())
                apart()
                dve.tensor_copy(mean[:, ds(first, n)], mv[:, 0:n, 0]).then_inc(st_step, st.one())
                dve.tensor_scalar(veps[:, ds(first, n)], mv[:, 0:n, 1], EPS, None, ALU.add).then_inc(veps_ready, 1)

            def normed(dst, i, n_rstd, signal):
                dve.wait_ge(rstd_ready, n_rstd)
                for t in range(TB):
                    dve.tensor_scalar(dst[:, t, :], tile(i + t), mean[:, ds(i + t, 1)], rstd[:, ds(i + t, 1)],
                                      ALU.subtract, ALU.mult).then_inc(signal, 1)

            dve.wait_ge(pads_ready, 2)
            for h in range(2):
                two = slice(2 * h, 2 * h + 2)
                dve.wait_ge(in_ps, 2 * h + 1)
                dve.tensor_copy(xpad[:, 0, two, DC - 1:PAD],
                                front_ps[:, 0, h * 512:h * 512 + 512].rearrange("p (b s) -> p b s", b=2))\
                    .then_inc(front_step, front.one())
                dve.wait_ge(front_step, front.now())
                dve.wait_ge(ld_small, 32)
                for c in range(NC):
                    if c == 1:
                        dve.wait_ge(xpad_ready, h + 1)
                    dve.tensor_scalar(conv[:, c, two, :], xpad[:, c, two, 0:S], conv_w[:, c, 0:1], None, ALU.mult)\
                        .then_inc(front_step, front.one())
                    for k in range(1, DC):
                        dve.wait_ge(front_step, front.now())
                        ins = dve.scalar_tensor_tensor(conv[:, c, two, :], xpad[:, c, two, k:k + S], conv_w[:, c, k:k + 1],
                                                       conv[:, c, two, :], ALU.mult, ALU.add)
                        if k < DC - 1:
                            ins.then_inc(front_step, front.one())
                        else:
                            ins.then_inc(conv_ready, 1)

            def row_max(i):
                dve.wait_ge(e_ps, i + 1)
                dve.tensor_reduce(neg_max[:, :], mm_ps, axis=AX.X, op=ALU.max, negate=True).then_inc(max_ready, 1)

            def normalise(i):
                dve.wait_ge(exp_ready, i * TB + TB)
                dve.reciprocal(row_inv[:, :], row_sum[:, :]).then_inc(attn_step, attn.one())
                dve.wait_ge(attn_step, attn.now())
                for m in range(TB):
                    dve.tensor_scalar(att[:, m, :], att[:, m, :], row_inv[:, m:m + 1], None, ALU.mult).then_inc(att_ready, 1)

            def x1(i):
                dve.wait_ge(xm_ps, i + 1)
                dve.scalar_tensor_tensor(tile(i * TB, TB), ps[:, 5, :], gains[:, 0:1], tile(i * TB, TB),
                                         ALU.mult, ALU.add).then_inc(attn_step, attn.one())
                dve.wait_ge(attn_step, attn.now())
                sums(attn, attn_step, i * TB, TB)

            attn.begin(0)
            row_max(0)
            dve.wait_ge(ld_x, 16)
            sums(front, front_step, 0, NT)
            dve.wait_ge(ld_small2, 16 * 7)
            dve.wait_ge(consts_ready, 1)
            for c in range(NC):
                dve.tensor_scalar(ident_d[:, c, :], ident[:, :], Dp[:, c:c + 1], None, ALU.mult).then_inc(d_ready, 1)
            dve.tensor_scalar(half_gs[:, :], gate_s[:, :], 0.5, None, ALU.mult).then_inc(front_step, front.one())
            normed(xl, 0, 1, xl_ready)
            dve.wait_ge(gains_ready, 1)
            dve.tensor_scalar(dsg[:, :], down_s[:, :], gains[:, 2:3], None, ALU.mult).then_inc(dsg_ready, 1)
            for c in range(NC):
                dve.wait_ge(spe_ready, c + 1)
                dve.tensor_scalar(sp_w[:, c, :], sp_e[:, c, :], 1.0, None, ALU.add).then_inc(spw_ready, 1)

            normalise(0)
            for c in range(NC):
                dve.wait_ge(spw_ready, c + 1)
                dve.scalar_tensor_tensor(sp_e[:, c, :], sp_w[:, c, :], 1.0, sp_e[:, c, :], ALU.subtract, ALU.subtract)\
                    .then_inc(front_step, front.one())
            rounded = front.now()
            for c in range(NC):
                dve.wait_ge(spi_ready, c + 1)
                dve.wait_ge(front_step, rounded - NC + c + 1)
                dve.scalar_tensor_tensor(sp_e[:, c, :], sp_i[:, c, :], 1.0, sp_e[:, c, :], ALU.add, ALU.mult)\
                    .then_inc(front_step, front.one())
            x1(0)
            for c in range(NC):
                dve.wait_ge(spv_ready, c + 1)
                dve.wait_ge(front_step, rounded + c + 1)
                dve.scalar_tensor_tensor(sp_v[:, c, :], sp_e[:, c, :], -0.5, sp_v[:, c, :], ALU.mult, ALU.add)\
                    .then_inc(front_step, front.one())

            def softplus(c):
                dve.wait_ge(front_step, front.now())
                dve.wait_ge(spl_ready, c + 1)
                dve.tensor_tensor(delta[:, c, :], sp_l[:, c, :], sp_v[:, c, :], ALU.add).then_inc(delta_ready, 1)
                dve.wait_ge(delta_ready, c + 1)
                dve.tensor_tensor(du[:, c, :], delta[:, c, :], u[:, c, :], ALU.mult).then_inc(du_ready, 1)
                dve.wait_ge(du_ready, c + 1)

            normed(xl, 0, 2, xl2_ready)
            attn.end()
            softplus(0)
            dve.sem_inc(scanned, 1)
            softplus(1)
            dve.sem_inc(scanned, SLOTS - 1)

            def merged(b, more):
                def scan(k):
                    dve.wait_ge(da_ready, b * UNITS + k + 1)
                    dve.wait_ge(dbu_ready, b * UNITS + k + 1)
                    if k >= 2:
                        dve.wait_ge(hc_ready, b * UNITS + k - 1)
                    dve.tensor_tensor_scan(hs[:, k % 2, :], dA[:, k % SLOTS, :], dBu[:, k % SLOTS, :], 0.0,
                                           ALU.mult, ALU.add).then_inc(scanned, 1)

                def times_c(k):
                    state = k // NC
                    dve.wait_ge(c_loaded[state % 2], b * (NPB // 2 * 16) + 16 * (state // 2 + 1))
                    dve.wait_ge(scanned, b * UNITS + SLOTS + k + 1)
                    dve.wait_ge(y_added, b * (UNITS // 2) + (k // SLOTS) * 2 + k % 2 + 1)
                    dve.tensor_tensor(hc[:, k % SLOTS, :], hs[:, k % 2, :], cbc[:, state % 2, :], ALU.mult)\
                       .then_inc(hc_ready, 1)

                def hidden(i):
                    m, s = chunk(i), i % 2
                    dve.wait_ge(gate_act, b * (2 * NI) + 2 * i + 2)
                    dve.scalar_tensor_tensor(ga[0:m, s, :], th[0:m, s, :], 1.0, ga[0:m, s, :], ALU.add, ALU.mult)\
                       .then_inc(ga_scaled, 1)
                    dve.wait_ge(ga_scaled, b * NI + i + 1)
                    dve.scalar_tensor_tensor(hdn[0:m, i, :], ps[0:m, 6 + s, S:2 * S], up_s[0:m, i:i + 1], ga[0:m, s, :],
                                             ALU.mult, ALU.mult).then_inc(hdn_ready, 1)

                def x2(b):
                    feed.begin(b)
                    dve.wait_ge(down_ps, b + 1)
                    dve.tensor_tensor(tile(b * TB, TB), tile(b * TB, TB), ps[:, 6, :], ALU.add).then_inc(x2_ready, 1)
                    dve.wait_ge(x2_ready, b + 1)
                    sums(feed, feed_step, b * TB, TB)
                    feed.end()

                def gate_x(b):
                    dve.wait_ge(feed_step, feed.now())
                    normed(gated[:, :, ds(b * S, S)], b * TB, b * 2 + (4 if more else 3), zl_ready)

                if more:
                    attn.begin(b + 1)
                if more:
                    dve.wait_ge(xl2T_ps, b + 1)
                    normed(xl, (b + 1) * TB, 1, xl_ready)
                scan(0)
                hidden(0)
                times_c(0)
                scan(1)
                hidden(1)
                times_c(1)
                scan(2)
                hidden(2)
                scan(3)
                times_c(2)
                hidden(3)
                if more:
                    row_max(b + 1)
                times_c(3)
                scan(4)
                scan(5)
                if more:
                    normalise(b + 1)
                hidden(4)
                times_c(4)
                hidden(5)
                scan(6)
                times_c(5)
                times_c(6)
                scan(7)
                if more:
                    x1(b + 1)
                times_c(7)
                if more:
                    normed(xl, (b + 1) * TB, b * 2 + 3, xl2_ready)
                x2(b)
                gate_x(b)
                if more:
                    attn.end()
                dve.wait_ge(hc_ready, b * UNITS + UNITS)

            with dve.Fori(0, B - 1) as b:
                merged(b, True)
            merged(B - 1, False)

            def times_y(i):
                dve.wait_ge(sz_ready, 1 if i < B - 1 else 2)
                mine = gated[:, :, i * S:i * S + S]
                dve.tensor_tensor(mine, y_ps[:, :, i * S:i * S + S], mine, ALU.mult).then_inc(yz_ready, 1)

            def x3(i):
                dve.wait_ge(yzT_ps, i + 1)
                dve.scalar_tensor_tensor(tile(i * TB, TB), ps[:, GATE_BANKS[i], :], gains[:, 1:2], tile(i * TB, TB),
                                         ALU.mult, ALU.add).then_inc(keys_step, keys.one())

            dve.wait_ge(y_added, B * UNITS // 2 + 2)
            for i in range(B):
                times_y(i)
            dve.wait_ge(zl_ready, NT)
            x3(0)
            dve.wait_ge(keys_step, keys.now())
            sums(keys, keys_step, 0, TB)
            x3(1)
            normed(xl, 0, 2 * B + 2, xn_ready)
            for i in range(2, B):
                x3(i)
            dve.wait_ge(keys_step, keys.now())
            sums(keys, keys_step, TB, NT - TB)
            dve.wait_ge(keys_step, keys.now())

            def weigh(b, s):
                dve.wait_ge(g_ready, b * (ROWS // 2) + ROWS // 2)
                dve.wait_ge(w_ps, b * TB + s + 1)
                mine = GT[:, :, s * P:s * P + P].rearrange("p r (g j) -> p r g j", g=GROUPS)
                dve.tensor_tensor(mine, mine, W_ps.rearrange("p j g r -> p r g j"), ALU.mult)\
                   .then_inc(gw_ready, 1)

            def top_keys(i, s, between=None):
                tops.begin(i * TB + s)
                for side in range(2):
                    dve.wait_ge(sim_ready, i * 2 * TB + 2 * s + side + 1)
                    apart()
                    for n in range(side * H, side * H + H):
                        dve.max(top[:, n, :], sims[:, s, n, :]).then_inc(top_step, tops.one())
                tops_done = tops.now()
                dve.wait_ge(top_step, tops_done - H)
                apart()
                for n in range(H):
                    dve.max_index(topi[:, n, :], top[:, n, :], sims[:, s, n, :]).then_inc(top_step, tops.one())
                dve.wait_ge(top_step, tops_done)
                dve.tensor_tensor(cand[:, :, :, :], top[:, 0:H, :].unsqueeze(3).to_broadcast([P, H, K, K]),
                                  top[:, H:NS, :].unsqueeze(2).to_broadcast([P, H, K, K]), ALU.add)\
                    .then_inc(top_step, tops.one())
                cand_done = tops.now()
                for n in range(H, NS):
                    dve.max_index(topi[:, n, :], top[:, n, :], sims[:, s, n, :]).then_inc(top_step, tops.one())
                index_done = tops.now()
                dve.wait_ge(top_step, cand_done)
                apart()
                for h in range(H):
                    dve.max(best[:, h, :], cand[:, h, :, :]).then_inc(top_step, tops.one())
                best_done = tops.now()
                dve.wait_ge(top_step, index_done)
                dve.tensor_copy(topf[:, :, :], topi[:, :, :]).then_inc(top_step, tops.one())
                dve.wait_ge(top_step, best_done)
                apart()
                for h in range(H):
                    dve.max_index(pk[:, h, :], best[:, h, :], cand[:, h, :, :].rearrange("p a b -> p (a b)"))\
                        .then_inc(top_step, tops.one())
                pairs_done = tops.now()
                dve.tensor_scalar(V[:, 2, :], best[:, :, :].rearrange("p h k -> p (h k)"), 0.0, None, ALU.max)\
                    .then_inc(top_step, tops.one())
                if between is not None:
                    weigh(*between)
                dve.wait_ge(top_step, pairs_done)
                pk_v = pk[:, :, :].rearrange("p h k -> p (h k)")
                dve.tensor_single_scalar(pab[:, 0, :], pk_v, 3, ALU.logical_shift_right)
                dve.tensor_single_scalar(pab[:, 1, :], pk_v, K - 1, ALU.bitwise_and).then_inc(top_step, tops.one())
                dve.wait_ge(top_step, tops.now())
                dve.tensor_copy(pabf[:, :], pab[:, :, :].rearrange("p a n -> p (a n)"))\
                    .then_inc(top_step, tops.one())
                dve.wait_ge(top_step, tops.now())
                dve.tensor_tensor(eq[:, :, :, :], pabf[:, :].rearrange("p (n k) -> p n k", k=K).unsqueeze(3)
                                  .to_broadcast([P, NS, K, K]),
                                  iota_f[:, 0:K].unsqueeze(1).unsqueeze(1).to_broadcast([P, NS, K, K]), ALU.is_equal)\
                    .then_inc(top_step, tops.one())
                dve.wait_ge(top_step, tops.now())
                dve.tensor_tensor(eq[:, :, :, :], eq[:, :, :, :],
                                  topf[:, :, :].unsqueeze(2).to_broadcast([P, NS, K, K]), ALU.mult)\
                    .then_inc(top_step, tops.one())
                dve.wait_ge(top_step, tops.now())
                dve.tensor_reduce(picked[:, :], eq[:, :, :, :].rearrange("p n k a -> p (n k) a"), axis=AX.X, op=ALU.add)\
                    .then_inc(top_step, tops.one())
                dve.wait_ge(top_step, tops.now())
                dve.tensor_scalar(over[:, :], picked[:, 0:HK], float(ROWS), float(NK - 1), ALU.is_ge, ALU.mult)\
                    .then_inc(top_step, tops.one())
                dve.tensor_scalar(V[:, 0, :], picked[:, 0:HK], float(ROWS - 1), None, ALU.min)\
                    .then_inc(top_step, tops.one())
                dve.wait_ge(top_step, tops.now())
                dve.tensor_tensor(V[:, 1, :], picked[:, HK:2 * HK], over[:, :], ALU.max)\
                    .then_inc(top_step, tops.one())
                dve.wait_ge(top_step, tops.now())
                dve.transpose(VT[:, :, :].rearrange("p q n -> p (q n)"), V[:, :, :].rearrange("p q n -> p (q n)"))\
                    .then_inc(top_step, tops.one())
                dve.wait_ge(top_step, tops.now())
                dve.tensor_copy(part[:, 0, :], VT[:, 2, :]).then_inc(top_step, tops.one())
                dve.tensor_copy(keys_b[:, :, :], VT[:, 0:2, :]).then_inc(top_step, tops.one())
                dve.wait_ge(top_step, tops.now())
                dve.tensor_tensor(rest[:, :], VT[:, 2, :], part[:, 0, :], ALU.subtract).then_inc(top_step, tops.one())
                rested = tops.now()
                dve.tensor_tensor(onehot1, iota_k[:, 0:ROWS, :], keys_b[:, 0, :].unsqueeze(1).to_broadcast([P, ROWS, HK]),
                                  ALU.is_equal).then_inc(top_step, tops.one())
                dve.wait_ge(top_step, rested)
                dve.tensor_copy(part[:, 1, :], rest[:, :]).then_inc(top_step, tops.one())
                dve.wait_ge(top_step, tops.now())
                dve.tensor_tensor(rest[:, :], rest[:, :], part[:, 1, :], ALU.subtract).then_inc(top_step, tops.one())
                rested = tops.now()
                dve.tensor_tensor(Y[:, s], iota_k, keys_b[:, 1, :].unsqueeze(1).to_broadcast([P, NK, HK]),
                                  ALU.is_equal).then_inc(top_step, tops.one())
                dve.wait_ge(top_step, rested)
                dve.tensor_copy(part[:, 2, :], rest[:, :]).then_inc(top_step, tops.one())
                dve.wait_ge(top_step, tops.now())
                dve.tensor_tensor(WG[:, :, :, :], part[:, :, :].unsqueeze(2).to_broadcast([P, PARTS, GROUPS, HK]),
                                  group[:, :, :].unsqueeze(1).to_broadcast([P, PARTS, GROUPS, HK]), ALU.mult)\
                    .then_inc(top_step, tops.one())
                dve.wait_ge(top_step, tops.now())
                for q in range(PARTS):
                    last = dve.tensor_tensor(XW[:, s, q], onehot1.unsqueeze(1).to_broadcast([P, GROUPS, ROWS, HK]),
                                             WG[:, q].unsqueeze(2).to_broadcast([P, GROUPS, ROWS, HK]), ALU.mult)
                last.then_inc(xw_ready, 1)
                tops.end()

            def finish(b, s):
                dve.wait_ge(up_ps, b * TB + s + 1)
                dve.wait_ge(stored, b * (16 * TB) + 1)
                apart()
                dve.scalar_tensor_tensor(fin[:, s, :], out_ps[s], gains[:, 3:4], tile(b * TB + s), ALU.mult, ALU.add)\
                   .then_inc(fin_ready, 1)

            def experts(b, more, early=False):
                if more:
                    dve.wait_ge(xnT_ps, b + 1)
                    normed(xl, (b + 1) * TB, 2 * B + 3, xn_ready)
                if early:
                    top_keys(b, 1, between=(b, 0))
                else:
                    top_keys(b, 1)
                    weigh(b, 0)
                weigh(b, 1)
                if more:
                    top_keys(b + 1, 0)
                finish(b, 0)
                finish(b, 1)

            dve.wait_ge(iota_ready, 1 + GROUPS)
            dve.wait_ge(iota_k_ready, 1)
            top_keys(0, 0)
            experts(0, True, early=True)
            with dve.Fori(1, B - 1) as b:
                experts(b, True)
            experts(B - 1, False)

        @block.tensor
        def _(pe):
            def turn(dst, src, signal):
                for i in range(2):
                    for j in range(2):
                        last = pe.transpose(dst[:, j, i * P:i * P + P], src[:, i, j * P:j * P + P], ident[:, :])
                last.then_inc(signal, 1)

            pe.wait_ge(ld_front, 32)
            for h in range(2):
                if h == 1:
                    pe.wait_ge(ld_front2, 16)
                for c in range(NC):
                    pe.matmul(front_ps[:, c, h * 512:h * 512 + 512], in_w[:, c * P:c * P + P], ctxT[:, h * 512:h * 512 + 512],
                              start=True, stop=True).then_inc(in_ps, 1)

            def project(i):
                pe.matmul(mm_ps[:, 0, :], wqT[:, :], ctxT[:, ds(i * S, S)], start=True, stop=True)
                pe.matmul(mm_ps[:, 1, :], wkT[:, :], ctxT[:, ds(i * S, S)], start=True, stop=True).then_inc(qk_ps, 1)

            def turn_xl(i):
                pe.wait_ge(xl_ready, i * TB + TB)
                turn(T_ps, xl, xlT_ps)

            def energy(i):
                pe.wait_ge(qk_ready, i * 2 + 2)
                for m in range(TB):
                    last = pe.matmul(mm_ps[:, m, :], qT[:, m * P:m * P + P], kT[:, :], start=True, stop=True)
                last.then_inc(e_ps, 1)

            def turn_att(i):
                pe.wait_ge(att_ready, i * TB + TB)
                pe.wait_ge(xlT_ready, i + 1)
                turn(T_ps, att, attT_ps)

            def mix(i):
                pe.wait_ge(attT_ready, i + 1)
                for l in range(TB):
                    for k in range(TB):
                        last = pe.matmul(mm_ps[:, l, :], xlT[:, k, l * P:l * P + P], attT[:, k, :],
                                         start=(k == 0), stop=(k == TB - 1))
                last.then_inc(xm_ps, 1)

            def turn_x2(i):
                pe.wait_ge(xl2_ready, i * TB + TB)
                turn(T_ps, xl, xl2T_ps)

            pe.wait_ge(ld_attn, 64)
            project(0)
            energy(0)
            pe.wait_ge(ld_xp, 32)
            for h in range(2):
                for c in range(NC):
                    pe.wait_ge(u_ready, h * NC + c + 1)
                    last = pe.matmul(ps[0:XD, 6 + h, :], xp_w[:, c, :], u[:, c, h * 512:h * 512 + 512],
                                     start=(c == 0), stop=(c == NC - 1))
                last.then_inc(xd_ps, 1)
                pe.wait_ge(xd_ready, h + 1)
                for c in range(NC):
                    pe.matmul(front_ps[:, c, h * 512:h * 512 + 512], dt_w[:, c * P:c * P + P], xdbl[0:DR, h * 512:h * 512 + 512],
                              start=True, stop=True).then_inc(dt_ps, 1)
            pe.wait_ge(consts_ready, 1)
            turn_xl(0)
            turn_att(0)
            mix(0)
            pe.wait_ge(spv_ready, NC)
            pe.wait_ge(d_ready, NC)
            for c in range(NC):
                for h in range(2):
                    pe.matmul(y_ps[:, c, h * 512:h * 512 + 512], ident_d[:, c, :], u[:, c, h * 512:h * 512 + 512],
                              start=True, stop=False, skip_group_check=True)
            turn_x2(0)
            pe.wait_ge(ld_ffn, 64)
            pe.wait_ge(down_w_ready, 2)
            pe.sem_inc(y_added, 2)

            def merged(b, more):
                def add_y(j):
                    pe.wait_ge(paired, b * (UNITS // 2) + j + 1)
                    c = j % 2
                    for h in range(2):
                        last = pe.matmul(y_ps[:, c, h * 512:h * 512 + 512], ident[:, :], hc[:, c, h * 512:h * 512 + 512],
                                         start=False, stop=False, skip_group_check=True)
                    last.then_inc(y_added, 1)

                def gate_up(i):
                    m, s = chunk(i), i % 2
                    if i >= 2:
                        pe.wait_ge(hdn_ready, b * NI + i - 1)
                    for n, w in enumerate((gate_w, up_w)):
                        for k in range(DK_F):
                            last = pe.matmul(ps[0:m, 6 + s, n * S:n * S + S], w[:, k, i * P:i * P + m], x2T[:, k, :],
                                             start=(k == 0), stop=(k == DK_F - 1))
                    last.then_inc(gu_ps, 1)

                def down(b):
                    pe.wait_ge(hdn_ready, b * NI + NI)
                    for t in range(TB):
                        for i in range(NI):
                            m = chunk(i)
                            last = pe.matmul(down_ps_v[:, t, :], hdn[0:m, i, t * P:t * P + P], down_w[0:m, i, :],
                                             start=(i == 0), stop=(i == NI - 1))
                    last.then_inc(down_ps, 1)

                pe.wait_ge(xl2T_ready, b + 1)
                gate_up(0)
                gate_up(1)
                if more:
                    project(b + 1)
                gate_up(2)
                gate_up(3)
                gate_up(4)
                if more:
                    energy(b + 1)
                    turn_xl(b + 1)
                gate_up(5)
                add_y(0)
                if more:
                    turn_att(b + 1)
                add_y(1)
                if more:
                    mix(b + 1)
                down(b)
                add_y(2)
                if more:
                    turn_x2(b + 1)
                add_y(3)
                pe.wait_ge(x2_ready, b + 1)

            with pe.Fori(0, B - 1) as b:
                merged(b, True)
            merged(B - 1, False)

            def gate_out(i):
                pe.wait_ge(yz_ready, i + 1 if i < 2 else B)
                turn(ps[:, GATE_BANKS[i], :].rearrange("p (k s) -> p k s", k=2), gated[:, :, i * S:i * S + S], yzT_ps)

            def scores(i, s):
                for side in range(2):
                    if s:
                        pe.wait_ge(sim_ready, i * 2 * TB + side + 1)
                    half = slice(side * DK, side * DK + DK)
                    for h in range(H):
                        if side == 0 and h % 2 == 0:
                            pe.wait_ge(q_ready, i * 2 + h // 2 + 1)
                        last = pe.matmul(ps[:, 5 + side, h * NK:h * NK + NK], qTp[half, h, s * P:s * P + P],
                                         keysT[half, h, :], start=True, stop=True)
                    last.then_inc(sim_ps, 1)

            def turn_xn(i):
                pe.wait_ge(xn_ready, i * TB + TB)
                turn(T_ps, xl, xnT_ps)

            def queries(i):
                pe.wait_ge(xnT_ready, i + 1)
                for n in range(2):
                    for h in range(2 * n, 2 * n + 2):
                        for k in range(DK_F):
                            last = pe.matmul(ps[:, 5 + n, (h % 2) * S:(h % 2) * S + S], wqp[:, k, h * P:h * P + P], xnT[:, k, :],
                                             start=(k == 0), stop=(k == DK_F - 1))
                    last.then_inc(q_ps, 1)

            def down(b, n):
                if n < 2:
                    pe.wait_ge(sim_ready, b * 2 * TB + 2 * TB - 1 + n)
                else:
                    pe.wait_ge(g_ready, b * (ROWS // 2) + n - 1)
                for r in range(2):
                    row = 2 * n + r
                    for k in range(DK_F):
                        last = pe.matmul(ps[:, 5 + n % 2, r * S:r * S + S], e_down[:, k, row * NK:row * NK + NK], xnT[:, k, :],
                                         start=(k == 0), stop=(k == DK_F - 1))
                last.then_inc(g_ps, 1)

            def weights(b, s):
                pe.wait_ge(xw_ready, b * TB + s + 1)
                if s:
                    pe.wait_ge(gw_ready, b * TB + s)
                for j in range(HK):
                    for q in range(PARTS):
                        last = pe.matmul(W_ps[:, j].rearrange("p g r -> p (g r)"), Y[:, s, :, j],
                                         XW[:, s, q, :, :, j].rearrange("p g r -> p (g r)"),
                                         start=(q == 0), stop=(q == PARTS - 1))
                last.then_inc(w_ps, 1)

            def up(b, s):
                pe.wait_ge(gw_ready, b * TB + s + 1)
                for r in range(ROWS):
                    last = pe.matmul(out_ps[s], GT[:, r, s * P:s * P + P], e_up[:, r, :], start=(r == 0), stop=(r == ROWS - 1))
                last.then_inc(up_ps, 1)

            def experts(b, more, early=False):
                for n in range(ROWS // 2):
                    down(b, n)
                if more:
                    turn_xn(b + 1)
                weights(b, 0)
                pe.wait_ge(g_ready, b * (ROWS // 2) + ROWS // 2)
                if more:
                    queries(b + 1)
                if early:
                    scores(b + 1, 0)
                    up(b, 0)
                    weights(b, 1)
                    scores(b + 1, 1)
                    up(b, 1)
                elif more:
                    weights(b, 1)
                    scores(b + 1, 0)
                    up(b, 0)
                    scores(b + 1, 1)
                    up(b, 1)
                else:
                    weights(b, 1)
                    up(b, 0)
                    up(b, 1)

            pe.wait_ge(ld_keys, 32)
            pe.wait_ge(ld_exp, 32)
            for i in range(B):
                gate_out(i)
            turn_xn(0)
            queries(0)
            scores(0, 0)
            scores(0, 1)
            experts(0, True, early=True)
            with pe.Fori(1, B - 1) as b:
                experts(b, True)
            experts(B - 1, False)


def columns(v, n):
    full = np.zeros((n * P,), v.dtype)
    full[:v.size] = v.reshape(-1)
    return np.ascontiguousarray(full.reshape(n, P).T)


def kernel(**inputs):
    import concourse.bacc as bacc
    from concourse.bass_utils import run_bass_kernel_spmd

    a = {k: np.asarray(v) for k, v in inputs.items()}
    t = lambda m: np.ascontiguousarray(m.T)
    arrays = {
        "x": np.ascontiguousarray(a["x"].reshape(T, D)),
        "ctxT": t(a["ctx_1024"].reshape(T, CTX)),
        "gates": np.concatenate([a["g_xattn"], a["g_ffn"]]).reshape(1, 4),
        "wqT": t(a["L0_xattn_Wq"]), "wkT": t(a["L0_xattn_Wk"]),
        "bq": a["L0_xattn_bq"].reshape(P, 1), "bk": a["L0_xattn_bk"].reshape(P, 1),
        "gate_wT": t(a["L0_ffn_gate_w"]), "up_wT": t(a["L0_ffn_up_w"]), "down_wT": t(a["L0_ffn_down_w"]),
        "gate_s": columns(a["L0_ffn_gate_s"], NI), "up_s": columns(a["L0_ffn_up_s"], NI),
        "down_s": a["L0_ffn_down_s"].reshape(1, D),
        "in_wT": t(a["L1_xattn_in_proj_w"]), "conv_w": a["L1_xattn_conv_w"],
        "conv_b": columns(a["L1_xattn_conv_b"], NC),
        "xp_wT": t(a["L1_xattn_x_proj_w"]), "dt_wT": t(a["L1_xattn_dt_proj_w"]),
        "dt_b": columns(a["L1_xattn_dt_proj_b"], NC), "A_log": a["L1_xattn_A_log"],
        "D": columns(a["L1_xattn_D"], NC),
        "wqp": a["L1_ffn_Wq"],
        "keysT": np.ascontiguousarray(a["L1_ffn_keys"].transpose(2, 3, 0, 1).reshape(2 * DK, H * NK)),
        "e_downT": t(a["L1_ffn_e_down"]), "e_up": a["L1_ffn_e_up"],
    }
    arrays = {k: np.ascontiguousarray(v) for k, v in arrays.items()}
    nc = bacc.Bacc("TRN2", target_bir_lowering=False, num_devices=1)
    io = {k: nc.dram_tensor(k, v.shape, mybir.dt.float32, kind="ExternalInput").ap() for k, v in arrays.items()}
    out = nc.dram_tensor("out", (T, D), mybir.dt.float32, kind="ExternalOutput").ap()
    build(nc, io, out)
    got = run_bass_kernel_spmd(nc, [arrays], core_ids=[0]).results[0]["out"]
    return np.asarray(got).reshape(B, S, D)
```
